# Optimizing a Trainium2 kernel written in Bass

```python
import numpy as np
import jax
import jax.numpy as jnp

def _softmax(x, axis=-1):
    return jax.nn.softmax(x, axis=axis)

def _gelu(x):
    return jax.nn.gelu(x, approximate=True)

def _silu(x):
    return jax.nn.silu(x)

def _sigmoid(x):
    return jax.nn.sigmoid(x)

def _layernorm(x, axis=-1, eps=1e-05):
    m = jnp.mean(x, axis=axis, keepdims=True)
    v = jnp.var(x, axis=axis, keepdims=True)
    return (x - m) / jnp.sqrt(v + eps)

def _scatter_add(tgt, idx, src, axis=0):
    return tgt.at[idx].add(src)

def _segment_sum(src, seg, n):
    return jax.ops.segment_sum(src, seg, n)
kernel_name = 'mk_sandwich_d1_jaxref_r8_1c7572'

def setup_inputs(seed: int=0):
    np.random.seed(seed)
    _w = jnp.asarray

    def _L0_attn_setup():
        import math
        import jax, jax.numpy as jnp
        import numpy as np
        N_HEAD = 16
        key = jax.random.key(seed)
        k1, k2, k3, k4 = jax.random.split(key, 4)
        B, T, C, R = (4, 256, 128, 64)
        std = 0.02
        return {'hidden_states': jax.random.normal(k1, (B, T, C), dtype=jnp.float32), 'W_basis': jax.random.normal(k2, (R, C), dtype=jnp.float32) * std, 'W_v': jax.random.normal(k3, (C, C), dtype=jnp.float32) * std, 'b_v': jnp.zeros((C,), dtype=jnp.float32), 'W_o': jax.random.normal(k4, (C, C), dtype=jnp.float32) * std, 'b_o': jnp.zeros((C,), dtype=jnp.float32)}
    _L0_attn_in = _L0_attn_setup()

    def _L0_ffn_setup():
        import jax, jax.numpy as jnp
        import numpy as np
        H = 128
        I = 88
        E = 64
        TOP_K = 8
        NG = 8
        TOPK_GROUP = 4
        N_SHARED = 2
        ROUTED_SCALE = 2.5
        S_I = I * N_SHARED

        def _route(x, gate_w, gate_bias):
            T = x.shape[0]
            logits = x @ gate_w.T
            scores = jax.nn.sigmoid(logits)
            scores_for_choice = scores + gate_bias[None, :]
            grp = scores_for_choice.reshape(T, NG, E // NG)
            group_scores = jnp.sum(jax.lax.top_k(grp, 2)[0], axis=-1)
            _, gidx = jax.lax.top_k(group_scores, TOPK_GROUP)
            gmask = jnp.zeros((T, NG), dtype=scores.dtype).at[jnp.arange(T)[:, None], gidx].set(1.0)
            emask = jnp.repeat(gmask, E // NG, axis=1)
            masked = jnp.where(emask > 0, scores_for_choice, 0.0)
            _, topk_idx = jax.lax.top_k(masked, TOP_K)
            topk_w = jnp.take_along_axis(scores, topk_idx, axis=1)
            topk_w = topk_w / (jnp.sum(topk_w, axis=-1, keepdims=True) + 1e-20)
            topk_w = topk_w * ROUTED_SCALE
            rw = jnp.zeros((T, E), dtype=scores.dtype).at[jnp.arange(T)[:, None], topk_idx].add(topk_w)
            return rw

        def _mlp(x, gw, uw, dw):
            return jax.nn.silu(x @ gw.T) * (x @ uw.T) @ dw.T
        key = jax.random.key(seed)
        ks = jax.random.split(key, 10)
        sc = 0.02
        return {'hidden_states': jax.random.normal(ks[0], (1, 128, H), dtype=jnp.float32), 'gate_w': sc * jax.random.normal(ks[1], (E, H), dtype=jnp.float32), 'gate_bias': sc * jax.random.normal(ks[2], (E,), dtype=jnp.float32), 'Wg': sc * jax.random.normal(ks[3], (E, I, H), dtype=jnp.float32), 'Wu': sc * jax.random.normal(ks[4], (E, I, H), dtype=jnp.float32), 'Wd': sc * jax.random.normal(ks[5], (E, H, I), dtype=jnp.float32), 'Sg': sc * jax.random.normal(ks[6], (S_I, H), dtype=jnp.float32), 'Su': sc * jax.random.normal(ks[7], (S_I, H), dtype=jnp.float32), 'Sd': sc * jax.random.normal(ks[8], (H, S_I), dtype=jnp.float32)}
    _L0_ffn_in = _L0_ffn_setup()
    _d = {'L0_attn_hidden_states': _L0_attn_in['hidden_states'], 'L0_attn_W_basis': _L0_attn_in['W_basis'], 'L0_attn_W_v': _L0_attn_in['W_v'], 'L0_attn_b_v': _L0_attn_in['b_v'], 'L0_attn_W_o': _L0_attn_in['W_o'], 'L0_attn_b_o': _L0_attn_in['b_o'], 'L0_ffn_gate_w': _L0_ffn_in['gate_w'], 'L0_ffn_gate_bias': _L0_ffn_in['gate_bias'], 'L0_ffn_Wg': _L0_ffn_in['Wg'], 'L0_ffn_Wu': _L0_ffn_in['Wu'], 'L0_ffn_Wd': _L0_ffn_in['Wd'], 'L0_ffn_Sg': _L0_ffn_in['Sg'], 'L0_ffn_Su': _L0_ffn_in['Su'], 'L0_ffn_Sd': _L0_ffn_in['Sd']}
    _x0 = _d['L0_attn_hidden_states']
    _d['L0_attn_hidden_states'] = jax.random.normal(jax.random.fold_in(jax.random.key(seed), 1), (2, 1024, 128), dtype=_x0.dtype)
    del _x0
    return _d

def reference(L0_attn_hidden_states, L0_attn_W_basis, L0_attn_W_v, L0_attn_b_v, L0_attn_W_o, L0_attn_b_o, L0_ffn_gate_w, L0_ffn_gate_bias, L0_ffn_Wg, L0_ffn_Wu, L0_ffn_Wd, L0_ffn_Sg, L0_ffn_Su, L0_ffn_Sd):

    def _L0_attn_ref(hidden_states, W_basis, W_v, b_v, W_o, b_o):
        import math
        import jax, jax.numpy as jnp
        import numpy as np
        N_HEAD = 16
        B, T, C = hidden_states.shape
        nh = N_HEAD
        hd = C // nh
        R = W_basis.shape[0]
        latent = hidden_states @ W_basis.T
        v = hidden_states @ W_v.T + b_v
        v = v.reshape(B, T, nh, hd).transpose(0, 2, 1, 3)
        scores = jnp.einsum('bqr,bkr->bqk', latent, latent) * (1.0 / math.sqrt(R))
        causal = jnp.tril(jnp.ones((T, T), dtype=bool))
        scores = jnp.where(causal[None, :, :], scores, -jnp.inf)
        att = jax.nn.softmax(scores, axis=-1)
        y = jnp.einsum('bqk,bhkd->bhqd', att, v)
        y = y.transpose(0, 2, 1, 3).reshape(B, T, C)
        out = y @ W_o.T + b_o
        return out

    def _L0_ffn_ref(hidden_states, gate_w, gate_bias, Wg, Wu, Wd, Sg, Su, Sd):
        import jax, jax.numpy as jnp
        import numpy as np
        H = 128
        I = 88
        E = 64
        TOP_K = 8
        NG = 8
        TOPK_GROUP = 4
        N_SHARED = 2
        ROUTED_SCALE = 2.5
        S_I = I * N_SHARED

        def _route(x, gate_w, gate_bias):
            T = x.shape[0]
            logits = x @ gate_w.T
            scores = jax.nn.sigmoid(logits)
            scores_for_choice = scores + gate_bias[None, :]
            grp = scores_for_choice.reshape(T, NG, E // NG)
            group_scores = jnp.sum(jax.lax.top_k(grp, 2)[0], axis=-1)
            _, gidx = jax.lax.top_k(group_scores, TOPK_GROUP)
            gmask = jnp.zeros((T, NG), dtype=scores.dtype).at[jnp.arange(T)[:, None], gidx].set(1.0)
            emask = jnp.repeat(gmask, E // NG, axis=1)
            masked = jnp.where(emask > 0, scores_for_choice, 0.0)
            _, topk_idx = jax.lax.top_k(masked, TOP_K)
            topk_w = jnp.take_along_axis(scores, topk_idx, axis=1)
            topk_w = topk_w / (jnp.sum(topk_w, axis=-1, keepdims=True) + 1e-20)
            topk_w = topk_w * ROUTED_SCALE
            rw = jnp.zeros((T, E), dtype=scores.dtype).at[jnp.arange(T)[:, None], topk_idx].add(topk_w)
            return rw

        def _mlp(x, gw, uw, dw):
            return jax.nn.silu(x @ gw.T) * (x @ uw.T) @ dw.T
        B, S, _ = hidden_states.shape
        x = hidden_states.reshape(B * S, H)
        rw = _route(x, gate_w, gate_bias)
        expert_out = jax.vmap(lambda gw_, uw_, dw_: _mlp(x, gw_, uw_, dw_))(Wg, Wu, Wd)
        routed = jnp.einsum('eth,te->th', expert_out, rw)
        shared = _mlp(x, Sg, Su, Sd)
        out = (routed + shared).reshape(B, S, H)
        return out
    x = L0_attn_hidden_states
    x = x + _layernorm(_L0_attn_ref(_layernorm(x, axis=-1), L0_attn_W_basis, L0_attn_W_v, L0_attn_b_v, L0_attn_W_o, L0_attn_b_o), axis=-1)
    x = x + _layernorm(_L0_ffn_ref(_layernorm(x, axis=-1), L0_ffn_gate_w, L0_ffn_gate_bias, L0_ffn_Wg, L0_ffn_Wu, L0_ffn_Wd, L0_ffn_Sg, L0_ffn_Su, L0_ffn_Sd), axis=-1)
    return x

_drawn_inputs = setup_inputs


def setup_inputs(seed=0):
    import zlib

    import numpy as np

    out = dict(_drawn_inputs(seed))
    spreads = {'L0_attn_b_v': (0.0, 0.1), 'L0_attn_b_o': (0.0, 0.1)}
    factors = {'L0_attn_W_basis': 3.351}
    for name, (base, spread) in spreads.items():
        noise = np.random.default_rng([zlib.crc32(name.encode()), seed]).standard_normal(out[name].shape)
        drawn = base * np.exp(spread * noise) if base else spread * noise
        out[name] = jnp.asarray(drawn.astype(out[name].dtype))
    for name, factor in factors.items():
        out[name] = (out[name] * factor).astype(out[name].dtype)
    return out
```

```python
from contextlib import ExitStack

import numpy as np

import concourse.bass as bass
from concourse import mybir

F32 = mybir.dt.float32
F32R = mybir.dt.float32r
ACT = mybir.ActivationFunctionType
ALU = mybir.AluOpType
AX = mybir.AxisListType

P = 128
EXPERTS = 64
GROUPS = 8
TOP_GROUPS = 4
ROUTED_SCALE = 2.5
EPS = 1e-5
MASKED = -1e30
TAKEN = -3e38
PACK = 8
PER_CHUNK = P // PACK


def build(nc, x, w_basis_t, w_v_t, b_v, w_o_t, b_o, gate_w_t, gate_bias, w_experts, w_shared_up,
          w_shared_down, out):
    batches, seq, C = x.shape
    R = w_basis_t.shape[1]
    TILES = batches * seq // P
    QUADS = TILES // 4
    QPB = seq // 512
    TPB = seq // P
    ROUNDS, SETS = w_experts.shape[0], w_experts.shape[1]
    SHARED, _, TWO_S = w_shared_up.shape
    SROWS = TWO_S // 2
    SCALE = 1.0 / float(R) ** 0.5
    E = EXPERTS
    GE = E // GROUPS
    assert C == P and QPB == 2 and SETS * PER_CHUNK == E and QUADS == 4

    x_tiles = x.rearrange("b (t p) c -> p (b t) c", p=P)
    out_tiles = out.rearrange("b (t p) c -> p (b t) c", p=P)

    with ExitStack() as ctx:
        def sb(name, shape, dt=F32):
            return ctx.enter_context(nc.sbuf_tensor(name, shape, dt))

        def sem(name):
            return ctx.enter_context(nc.semaphore(name))

        ps = ctx.enter_context(nc.psum_tensor("ps", [P, 8, 512], F32))

        ident = sb("ident", [P, P])
        ident_r = sb("ident_r", [P, P], F32R)
        mask_f = sb("mask_f", [P, 2, P])
        masks = sb("masks", [P, 2, P], F32R)
        mask_rows = masks[:, 0, :]
        mask_cols = masks[:, 1, :]
        pick_f = sb("pick_f", [P, P])
        pick = sb("pick", [P, P], F32R)
        lower = sb("lower", [P, GROUPS, GROUPS])
        wb_sb = sb("wb_sb", [P, 2 * R])
        wv_sb = sb("wv_sb", [P, P])
        wo_sb = sb("wo_sb", [P, P])
        gw_sb = sb("gw_sb", [P, E])
        bv_sb = sb("bv_sb", [P, 1])
        bo_sb = sb("bo_sb", [P, P])
        gb_sb = sb("gb_sb", [P, E])
        x_sb = sb("x_sb", [P, TILES, C])
        x1_sb = sb("x1_sb", [P, TILES, C])
        stats = sb("stats", [P, 4, 6])
        mv = sb("mv", [P, 4, 2])
        rstd = sb("rstd", [P, 4])
        var_e = sb("var_e", [P, 4])
        minus_half = sb("minus_half", [P, 4])
        xn = sb("xn", [P, 2, 4, C])
        xn_t = sb("xn_t", [P, 2, 512])
        lat_hi = sb("lat_hi", [P, TILES * P], F32R)
        lat_lo = sb("lat_lo", [P, TILES * P], F32R)
        lat_hl = sb("lat_hl", [P, TILES * P], F32R)
        neg_max_t = sb("neg_max_t", [P, 2, 512], F32R)
        v_t = sb("v_t", [P, 2, 512])
        vals = sb("vals", [P, TILES, C + 4])
        neg_max = sb("neg_max", [P, TILES])
        arena = sb("arena", [P, 2 * TPB * 512])
        exp_t = arena[:, :].rearrange("p (k j n) -> p k j n", k=2, j=TPB)
        half = TPB * 512
        y_t = arena[:, half:half + 512 * QUADS].rearrange("p (q n) -> p q n", n=512)
        half += 512 * QUADS
        gated = arena[:, half:half + 1024].rearrange("p (k n) -> p k n", k=2)
        up_w = arena[:, half + 1024:half + 2048].rearrange("p (k n) -> p k n", k=2)
        row_sum_inv = sb("row_sum_inv", [P, TILES])
        att = sb("att", [P, 2, 4, C])
        xn2 = sb("xn2", [P, 4, C])
        x2_t = sb("x2_t", [P, 512])
        x_hi = sb("x_hi", [P, TILES * P], F32R)
        x_lo = sb("x_lo", [P, TILES * P], F32R)
        scores = sb("scores", [P, 2, 4, E])
        choice = sb("choice", [P, 4, E])
        big = [sb(f"big{n}", [P, 4 * GROUPS, 4 >> n]) for n in range(3)]
        small = [sb(f"small{n}", [P, 4 * GROUPS, 4 >> n]) for n in range(3)]
        low_big = sb("low_big", [P, 4 * GROUPS, 2])
        group_score = sb("group_score", [P, 4, GROUPS])
        above = sb("above", [P, 4, GROUPS, GROUPS])
        equal = sb("equal", [P, 4, GROUPS, GROUPS])
        group_rank = sb("group_rank", [P, 4, GROUPS])
        group_in = sb("group_in", [P, 4, GROUPS])
        masked = sb("masked", [P, 4, E])
        top8 = sb("top8", [P, 4, 8])
        left = sb("left", [P, 4, E])
        route = sb("route", [P, 4, E])
        route_x = sb("route_x", [P, 4, E, PACK])
        wsum = sb("wsum", [P, 4])
        winv = sb("winv", [P, 4])
        route_w = sb("route_w", [P, SETS, TILES * P])
        sh_raw = sb("sh_raw", [P, SHARED, 3 * P])
        sh_hi = sb("sh_hi", [P, SHARED, 3 * P], F32R)
        sh_lo = sb("sh_lo", [P, SHARED, 3 * P], F32R)
        w_raw = sb("w_raw", [P, SETS, 3 * P])
        w_hi = sb("w_hi", [P, SETS, 3 * P], F32R)
        w_lo = sb("w_lo", [P, SETS, 3 * P], F32R)
        hid = arena[:, 0:1024].rearrange("p (k n) -> p k n", k=2)
        hid_hi = lat_hl[:, 0:1024].rearrange("p (k n) -> p k n", k=2)
        hid_lo = lat_hl[:, 1024:2048].rearrange("p (k n) -> p k n", k=2)

        s_x = [sem(f"x_loaded{q}") for q in range(QUADS)]
        s_w = sem("small_weights_loaded")
        s_const = sem("constants_made")
        s_pool = sem("pool_step")
        s_dve = sem("dve_step")
        s_act = sem("act_step")
        s_var = sem("variance_ready")
        s_rstd = sem("rstd_ready")
        s_scaled = sem("norm_scaled")
        s_xn_tp = sem("xn_transposed_psum")
        s_xn_t = sem("xn_t_ready")
        s_lat = sem("latent_psum")
        s_lhi = sem("lat_hi_ready")
        s_llo = sem("lat_lo_ready")
        s_vtp = sem("v_t_psum")
        s_vt = sem("v_t_ready")
        s_vp = sem("vals_psum")
        s_v = sem("vals_ready")
        s_rows = sem("score_rows_psum")
        s_max = sem("row_max_ready")
        s_mrow = sem("max_row_psum")
        s_mhi = sem("neg_max_hi_ready")
        s_mlo = sem("neg_max_t_ready")
        s_cols = sem("score_cols_psum")
        s_exp = sem("exp_ready")
        s_pv = sem("att_psum")
        s_att = sem("att_ready")
        s_x1 = sem("x1_ready")
        s_x2p = sem("x2_t_psum")
        s_x2 = sem("x2_t_ready")
        s_xhi = sem("x_hi_ready")
        s_xlo = sem("x_lo_ready")
        s_lg = sem("logits_psum")
        s_sc = sem("scores_ready")
        s_route = sem("route_ready")
        s_rx = sem("route_x_ready")
        s_rtp = sem("route_t_psum")
        s_rw = sem("route_w_ready")
        s_wl = [sem(f"expert_w_loaded{k}") for k in range(SETS)]
        s_shl = sem("shared_w_loaded")
        s_shhi = sem("shared_hi_ready")
        s_shlo = sem("shared_lo_ready")
        s_whi = sem("w_hi_ready")
        s_wlo = sem("w_lo_ready")
        s_gate = sem("gate_psum")
        s_up = sem("up_psum")
        s_gated = sem("gated_ready")
        s_upw = sem("up_weighted")
        s_hid = sem("hidden_ready")
        s_hhi = sem("hidden_hi_ready")
        s_hlo = sem("hidden_lo_ready")
        s_down = sem("down_done")
        s_yt = sem("y_t_ready")
        s_yp = sem("y_psum")
        s_y = sem("y_ready")
        s_out = sem("out_stored")

        W_LOADS = 8
        def A(q):
            return [("A", q, r) for r in range(4)]

        def B(q):
            return [("M", q, 0)] + [("B", q, j) for j in range(4 * (q % QPB) + 4)]

        def one(names):
            return [(n[0], int(n[1]), h) for n in names.split() for h in range(1 + (n[0] == "C"))]

        def mix(long, short):
            out_, k = [], 0
            for n, st in enumerate(long):
                out_.append(st)
                while k < len(short) and (k + 1) * len(long) <= (n + 1) * len(short):
                    out_.append(short[k])
                    k += 1
            return out_ + short[k:]

        ORDER = (one("P0 P1 Q0 P2 Q1 V0") + A(0) + one("P3 Q2 V1") + mix(B(0), A(1))
                 + one("Q3 V2") + one("C0") + mix(B(1), A(2)) + one("V3 D0 C1") + mix(B(2), A(3))
                 + one("E0 D1 C2") + B(3)
                 + one("E1 H0 D2 C3 K0 E2 D3 G0 H1 E3 K1 G1 H2 K2 G2 H3 K3 G3"))

        def keys_of(q):
            return 4 * (q % QPB) + 4

        def cols_before(q):
            return sum(keys_of(k) for k in range(q))

        def stage_before(at, kinds):
            found = [st for st in ORDER[:at] if st[0] in kinds]
            return found[-1] if found else None

        def norm_of(kind, q):
            return sum({"P": 1, "D": 2}.get(st[0], 0) for st in ORDER[:ORDER.index((kind, q, 0))])

        NORMS = 3 * QUADS

        STEPS0 = 4 * SHARED
        PER_ROUND = 4 * SETS
        ALL_STEPS = STEPS0 + ROUNDS * PER_ROUND
        LAG = 2
        AHEAD = 2
        WD = 2 * P

        def later(s, n):
            return not isinstance(s, int) or s >= n

        block = ctx.enter_context(nc.Block())

        @block.sync
        def _(sp):
            sp.dma_start(x_sb[:, 0:4, :], x_tiles[:, 0:4, :]).then_inc(s_x[0], 16)
            for half in range(2):
                sp.dma_start(wb_sb[:, R * half:R * half + R], w_basis_t).then_inc(s_w, 16)
            sp.dma_start(wv_sb[:], w_v_t).then_inc(s_w, 16)
            sp.dma_start(wo_sb[:], w_o_t).then_inc(s_w, 16)
            sp.dma_start(bv_sb[:], b_v).then_inc(s_w, 16)
            sp.dma_start(bo_sb[:], b_o.to_broadcast([P, C])).then_inc(s_w, 16)
            sp.dma_start(gw_sb[:], gate_w_t).then_inc(s_w, 16)
            sp.dma_start(gb_sb[:], gate_bias.to_broadcast([P, E])).then_inc(s_w, 16)
            for q in range(1, QUADS):
                sp.dma_start(x_sb[:, 4 * q:4 * q + 4, :],
                             x_tiles[:, 4 * q:4 * q + 4, :]).then_inc(s_x[q], 16)
            for c in range(SHARED):
                sp.dma_start(sh_raw[:, c, 0:2 * SROWS], w_shared_up[c]).then_inc(s_shl, 16)
                sp.dma_start(sh_raw[0:SROWS, c, WD:WD + P], w_shared_down[c]).then_inc(s_shl, 16)
            for c in range(SETS):
                sp.dma_start(w_raw[:, c, :], w_experts[0, c]).then_inc(s_wl[c], 16)
            with sp.Fori(0, ROUNDS - 1) as r:
                for c in range(SETS):
                    sp.wait_ge(s_whi, r * SETS + (c + 1))
                    sp.wait_ge(s_wlo, r * SETS + (c + 1))
                    sp.dma_start(w_raw[:, c, :], w_experts[r + 1, c]).then_inc(s_wl[c], 16)
            for q in range(QUADS):
                sp.wait_ge(s_y, q + 1)
                sp.dma_start(out_tiles[:, 4 * q:4 * q + 4, :],
                             x_sb[:, 4 * q:4 * q + 4, :]).then_inc(s_out, 16)
            sp.wait_ge(s_out, 16 * QUADS)

        @block.gpsimd
        def _(pool):
            g = nc.gpsimd
            steps = [0]

            def link(ins):
                steps[0] += 1
                ins.then_inc(s_pool, 1)
                pool.wait_ge(s_pool, steps[0])

            g.memset(ident[:], 0.0)
            g.memset(minus_half[:], -0.5)
            g.memset(mask_f[:], 0.0)
            g.memset(lower[:], 0.0)
            g.memset(pick_f[:], 0.0)
            link(g.memset(vals[:, :, C:C + 4], 1.0))
            link(g.memset(pick_f[0:1, :], 1.0))
            link(g.memset(pick_f[R:R + 1, :], 1.0))
            g.affine_select(out=ident[:], in_=ident[:], compare_op=ALU.not_equal, fill=1.0, base=0,
                            pattern=[[-1, P]], channel_multiplier=1)
            g.affine_select(out=mask_f[:, 0, :], in_=mask_f[:, 0, :], compare_op=ALU.is_ge,
                            fill=MASKED, base=0, pattern=[[-1, P]], channel_multiplier=1)
            g.affine_select(out=mask_f[:, 1, :], in_=mask_f[:, 1, :], compare_op=ALU.is_ge,
                            fill=MASKED, base=0, pattern=[[1, P]], channel_multiplier=-1)
            link(g.affine_select(out=lower[:], in_=lower[:], compare_op=ALU.is_ge, fill=1.0,
                                 base=0, pattern=[[-1, GROUPS], [1, GROUPS]],
                                 channel_multiplier=0))
            g.tensor_copy(ident_r[:], ident[:])
            g.tensor_copy(pick[:], pick_f[:])
            g.tensor_copy(masks[:], mask_f[:]).then_inc(s_const, 1)

            def low_part(q):
                pool.wait_ge(s_x2, q + 1)
                pool.wait_ge(s_xhi, q + 1)
                g.tensor_tensor(x_lo[:, 512 * q:512 * q + 512], x2_t[:, :], x_hi[:, 512 * q:512 * q + 512],
                                ALU.subtract).then_inc(s_xlo, 1)

            def inv_sqrt(n):
                pool.wait_ge(s_var, n + 1)
                link(g.tensor_scalar(var_e[:], mv[:, :, 1], EPS, None, ALU.add))
                g.tensor_tensor(rstd[:], var_e[:], minus_half[:], ALU.pow).then_inc(s_rstd, 1)

            def scale(n, src, dst):
                inv_sqrt(n)
                pool.wait_ge(s_rstd, n + 1)
                for t in range(4):
                    ins = g.tensor_scalar(dst(t), src(t), mv[:, t, 0:1], rstd[:, t:t + 1],
                                          ALU.subtract, ALU.mult)
                ins.then_inc(s_scaled, 1)

            for what, q, _ in ORDER:
                if what == "P":
                    if q >= 2:
                        pool.wait_ge(s_xn_tp, q - 1)
                    scale(norm_of("P", q), lambda t: x_sb[:, 4 * q + t, :],
                          lambda t: xn[:, q % 2, t, :])
                elif what == "D":
                    own = slice(4 * q, 4 * q + 4)
                    if q >= 1:
                        pool.wait_ge(s_x2p, q)
                    n = norm_of("D", q)
                    scale(n, lambda t: att[:, q % 2, t, :], lambda t: xn2[:, t, :])
                    pool.wait_ge(s_scaled, n + 1)
                    g.tensor_tensor(x1_sb[:, own, :], xn2[:, :, :], x_sb[:, own, :],
                                    ALU.add).then_inc(s_x1, 1)
                    pool.wait_ge(s_x1, q + 1)
                    scale(n + 1, lambda t: x1_sb[:, 4 * q + t, :], lambda t: xn2[:, t, :])
                elif what == "E":
                    low_part(q)
            pool.wait_ge(s_pv, 2 * QUADS)
            link(g.memset(hid, 0.0))

            def hidden(k, s, rows=P):
                pool.wait_ge(s_gated, s + 1)
                pool.wait_ge(s_upw, s + 1)
                if later(s, 2):
                    pool.wait_ge(s_hlo, s - 1)
                g.tensor_tensor(hid[0:rows, k, :], gated[0:rows, k, :], up_w[0:rows, k, :],
                                ALU.mult).then_inc(s_hid, 1)

            for s in range(STEPS0):
                hidden(s % 2, s, SROWS)
            with pool.Fori(0, ROUNDS) as r:
                for k in range(PER_ROUND):
                    hidden(k % 2, r * PER_ROUND + (STEPS0 + k))
            for q in range(QUADS):
                inv_sqrt(NORMS + q)

        @block.scalar
        def _(act):
            a = nc.scalar

            def keep_xn_t(q):
                act.wait_ge(s_xn_tp, q + 1)
                if q >= 2:
                    act.wait_ge(s_vtp, q - 1)
                a.copy(xn_t[:, q % 2, :], ps[:, 0, :]).then_inc(s_xn_t, 1)

            def keep_latent(q):
                own = slice(512 * q, 512 * q + 512)
                act.wait_ge(s_lat, q + 1)
                a.copy(lat_hi[:, own], ps[:, 1, :])
                a.copy(lat_hl[0:R, own], ps[0:R, 1, :]).then_inc(s_lhi, 1)
                act.wait_ge(s_vtp, q + 1)
                act.wait_ge(s_w, 16 * W_LOADS)
                if q >= 2:
                    act.wait_ge(s_vp, q - 1)
                a.activation(v_t[:, q % 2, :], ps[:, 6, :], ACT.Identity,
                             bias=bv_sb[:, 0:1]).then_inc(s_vt, 1)

            def keep_values(q):
                act.wait_ge(s_vp, q + 1)
                a.copy(vals[:, 4 * q:4 * q + 4, 0:C],
                       ps[:, 7, :].rearrange("p (t c) -> p t c", t=4)).then_inc(s_v, 1)

            def max_row(q):
                act.wait_ge(s_mrow, q + 1)
                if q >= 2:
                    act.wait_ge(s_cols, cols_before(q - 1))
                a.copy(neg_max_t[:, q % 2, :], ps[:, 1, :]).then_inc(s_mhi, 1)

            def exp_cols(q, j):
                d = j - (keys_of(q) - 4)
                act.wait_ge(s_cols, cols_before(q) + j + 1)
                if q >= 2 and j == 0:
                    act.wait_ge(s_pv, 2 * q - 2)
                lo = P * max(d, 0)
                a.activation(exp_t[:, q % 2, j, lo:512],
                             ps[:, 4 + (cols_before(q) + j) % 2, lo:512], ACT.Exp,
                             scale=SCALE).then_inc(s_exp, 1)

            def expert_input(q):
                act.wait_ge(s_x2p, q + 1)
                if q >= 1:
                    act.wait_ge(s_lg, q)
                    act.wait_ge(s_xlo, q)
                a.copy(x2_t[:, :], ps[:, 0, :]).then_inc(s_x2, 1)
                a.copy(x_hi[:, 512 * q:512 * q + 512], ps[:, 0, :]).then_inc(s_xhi, 1)
                act.wait_ge(s_lg, q + 1)
                if q >= 2:
                    act.wait_ge(s_route, q - 1)
                a.activation(scores[:, q % 2].rearrange("p t e -> p (t e)"), ps[:, 1, 0:4 * E],
                             ACT.Sigmoid).then_inc(s_sc, 1)

            def repeat_route(q):
                act.wait_ge(s_route, q + 1)
                if q >= 1:
                    act.wait_ge(s_rtp, SETS * q)
                a.copy(route_x[:], route[:, :, :].unsqueeze(3).to_broadcast([P, 4, E, PACK])
                       ).then_inc(s_rx, 1)

            def keep_route(q):
                for g in range(SETS):
                    n = SETS * q + g
                    act.wait_ge(s_rtp, n + 1)
                    a.copy(route_w[:, g, 512 * q:512 * q + 512],
                           ps[:, 2 + n % 2, :]).then_inc(s_rw, 1)

            for what, q, n in ORDER:
                if what == "P":
                    keep_xn_t(q)
                elif what == "Q":
                    keep_latent(q)
                elif what == "V":
                    keep_values(q)
                elif what == "M":
                    max_row(q)
                elif what == "B":
                    exp_cols(q, n)
                elif what == "E":
                    expert_input(q)
                elif what == "K":
                    repeat_route(q)
                elif what == "G":
                    keep_route(q)

            def split_hi(c, n, loads):
                act.wait_ge(s_wl[c], loads)
                if later(n, SETS):
                    act.wait_ge(s_down, (n - (SETS - 1)) * 4 + STEPS0)
                a.copy(w_hi[:, c, :], w_raw[:, c, :]).then_inc(s_whi, 1)

            def gate(k, s, rows=P):
                act.wait_ge(s_gate, s + 1)
                if later(s, 2):
                    act.wait_ge(s_hid, s - 1)
                a.activation(gated[0:rows, k % 2, :], ps[0:rows, 2 * (k % 2), :],
                             ACT.Silu).then_inc(s_gated, 1)

            def hidden_hi(k, s):
                act.wait_ge(s_hid, s + 1)
                if later(s, 2):
                    act.wait_ge(s_down, s - 1)
                a.copy(hid_hi[:, k % 2, :], hid[:, k % 2, :]).then_inc(s_hhi, 1)

            act.wait_ge(s_shl, 16 * 2 * SHARED)
            for c in range(SHARED):
                a.copy(sh_hi[:, c, 0:2 * SROWS], sh_raw[:, c, 0:2 * SROWS]).then_inc(s_shhi, 1)
                a.copy(sh_hi[0:SROWS, c, WD:WD + P],
                       sh_raw[0:SROWS, c, WD:WD + P]).then_inc(s_shhi, 1)
            for c in range(AHEAD):
                split_hi(c, c, 16)
            for s in range(STEPS0):
                gate(s, s, SROWS)
                if s >= 1:
                    hidden_hi(s - 1, s - 1)

            def round_steps(r, last=False):
                for k in range(PER_ROUND):
                    s = r * PER_ROUND + (STEPS0 + k)
                    gate(k, s)
                    hidden_hi(k - 1, s - 1)
                    c = k // 4 + AHEAD
                    if k % 4 == 1 and not (last and c >= SETS):
                        split_hi(c % SETS, r * SETS + c, (r + (1 + c // SETS)) * 16)

            with act.Fori(0, ROUNDS - 1) as r:
                round_steps(r)
            round_steps(ROUNDS - 1, last=True)
            hidden_hi(ALL_STEPS - 1, ALL_STEPS - 1)
            for q in range(QUADS):
                act.wait_ge(s_down, ALL_STEPS - QUADS + q + 1)
                a.copy(y_t[:, q, :], ps[:, 4 + q, :]).then_inc(s_yt, 1)

        @block.vector
        def _(dve):
            v = nc.vector
            steps = [0]

            def link(ins):
                steps[0] += 1
                ins.then_inc(s_dve, 1)
                dve.wait_ge(s_dve, steps[0])

            def statistics(src):
                if norms_done[0]:
                    dve.wait_ge(s_scaled, min(norms_done[0], NORMS))
                norms_done[0] += 1
                for t in range(4):
                    ins = v.bn_stats(stats[:, t, :], src(t))
                link(ins)
                for t in range(4):
                    ins = v.bn_aggr(mv[:, t, :], stats[:, t, :])
                ins.then_inc(s_var, 1)

            norms_done = [0]

            def flat(t3):
                return t3.rearrange("p a b -> p (a b)")

            def latent_lo(q):
                own = slice(512 * q, 512 * q + 512)
                dve.wait_ge(s_lhi, q + 1)
                link(v.tensor_tensor(lat_lo[:, own], ps[:, 1, :], lat_hi[:, own], ALU.subtract))
                v.tensor_copy(lat_hl[R:2 * R, own], lat_lo[R:2 * R, own]).then_inc(s_llo, 1)

            def row_max(q, r):
                i = keys_of(q) - 4 + r
                first = 2 + (r % 2 if q % QPB == 0 else 0)
                rows = ps[:, first:4, :].rearrange("p a b -> p (a b)")
                dve.wait_ge(s_rows, 4 * q + r + 1)
                v.tensor_reduce(neg_max[:, 4 * q + r:4 * q + r + 1], rows[:, 0:P * i + P],
                                AX.X, ALU.max, negate=True).then_inc(s_max, 1)

            def max_row_lo(q):
                dve.wait_ge(s_mhi, q + 1)
                low = neg_max_t[R:P, q % 2, :]
                v.tensor_tensor(low, ps[R:P, 1, :], low, ALU.subtract).then_inc(s_mlo, 1)

            def divide(q, h):
                dve.wait_ge(s_pv, 2 * q + h + 1)
                bank = ps[:, 6 + h, :].rearrange("p (t c) -> p t c", t=2)
                inv = row_sum_inv[:, 4 * q + 2 * h:4 * q + 2 * h + 2]
                link(v.reciprocal(inv, bank[:, :, C]))
                for t in range(2):
                    ins = v.scalar_tensor_tensor(
                        out=att[:, q % 2, 2 * h + t, :], in0=bank[:, t, 0:C],
                        scalar=inv[:, t:t + 1], in1=bo_sb[:], op0=ALU.mult, op1=ALU.add)
                ins.then_inc(s_att, 1)

            def norm_stats(q):
                dve.wait_ge(s_att, 2 * q + 2)
                statistics(lambda t: att[:, q % 2, t, :])
                dve.wait_ge(s_x1, q + 1)
                statistics(lambda t: x1_sb[:, 4 * q + t, :])

            tt = v.tensor_tensor

            def choose_groups(q):
                k = q % 2
                dve.wait_ge(s_sc, q + 1)
                link(tt(choice[:], scores[:, k], gb_sb[:, :].unsqueeze(1).to_broadcast([P, 4, E]),
                        ALU.add))
                grp = choice[:, :, :].rearrange("p t (g k) -> p (t g) k", k=GE)
                tt(big[0][:], grp[:, :, 0:4], grp[:, :, 4:8], ALU.max)
                link(tt(small[0][:], grp[:, :, 0:4], grp[:, :, 4:8], ALU.min))
                for n in range(2):
                    w = 2 >> n
                    b0, b1 = big[n][:, :, 0:w], big[n][:, :, w:2 * w]
                    tt(big[n + 1][:], b0, b1, ALU.max)
                    tt(low_big[:, :, 0:w], b0, b1, ALU.min)
                    link(tt(small[n + 1][:], small[n][:, :, 0:w], small[n][:, :, w:2 * w],
                            ALU.max))
                    link(tt(small[n + 1][:], small[n + 1][:], low_big[:, :, 0:w], ALU.max))
                link(tt(group_score[:, :, :].rearrange("p t g -> p (t g)"), big[2][:, :, 0],
                        small[2][:, :, 0], ALU.add))
                of_g = group_score[:, :, :].unsqueeze(3).to_broadcast([P, 4, GROUPS, GROUPS])
                of_h = group_score[:, :, :].unsqueeze(2).to_broadcast([P, 4, GROUPS, GROUPS])
                tt(above[:], of_h, of_g, ALU.is_gt)
                link(tt(equal[:], of_h, of_g, ALU.is_equal))
                link(tt(equal[:], equal[:],
                        lower[:, :, :].unsqueeze(1).to_broadcast([P, 4, GROUPS, GROUPS]),
                        ALU.mult))
                link(tt(above[:], above[:], equal[:], ALU.add))
                link(v.tensor_reduce(group_rank[:], above[:], AX.X, ALU.add))
                link(v.tensor_scalar(group_in[:], group_rank[:], TOP_GROUPS - 0.5, None, ALU.is_lt))
                link(tt(masked[:].rearrange("p t (g k) -> p t g k", k=GE),
                   choice[:, :, :].rearrange("p t (g k) -> p t g k", k=GE),
                   group_in[:, :, :].unsqueeze(3).to_broadcast([P, 4, GROUPS, GE]),
                   ALU.mult))

            def choose_experts(q):
                k = q % 2
                for t in range(4):
                    ins = v.max(top8[:, t, :], masked[:, t, :])
                link(ins)
                for t in range(4):
                    ins = v.match_replace(left[:, t, :], top8[:, t, :], masked[:, t, :], TAKEN)
                link(ins)
                link(v.tensor_tensor(left[:], left[:], masked[:], ALU.not_equal))
                link(v.tensor_tensor(left[:], left[:], scores[:, k], ALU.mult))
                link(v.tensor_reduce(wsum[:], left[:], AX.X, ALU.add))
                link(v.tensor_scalar(wsum[:], wsum[:], 1e-20, None, ALU.add))
                link(v.reciprocal(winv[:], wsum[:]))
                link(v.tensor_scalar(winv[:], winv[:], ROUTED_SCALE, None, ALU.mult))
                if q >= 1:
                    dve.wait_ge(s_rx, q)
                v.tensor_tensor(route[:], left[:],
                                winv[:, :].unsqueeze(2).to_broadcast([P, 4, E]),
                                ALU.mult).then_inc(s_route, 1)

            dve.wait_ge(s_w, 16 * W_LOADS)
            for what, q, n in ORDER:
                if what == "P":
                    dve.wait_ge(s_x[q], 16)
                    statistics(lambda t: x_sb[:, 4 * q + t, :])
                elif what == "Q":
                    latent_lo(q)
                elif what == "A":
                    row_max(q, n)
                elif what == "M":
                    max_row_lo(q)
                elif what == "C":
                    divide(q, n)
                elif what == "D":
                    norm_stats(q)
                elif what == "H":
                    choose_groups(q)
                    choose_experts(q)

            def split_lo(c, n, loads):
                dve.wait_ge(s_wl[c], loads)
                dve.wait_ge(s_whi, n + 1)
                if later(n, SETS):
                    dve.wait_ge(s_down, (n - (SETS - 1)) * 4 + STEPS0)
                v.tensor_tensor(w_lo[:, c, :], w_raw[:, c, :], w_hi[:, c, :],
                                ALU.subtract).then_inc(s_wlo, 1)

            def weigh(k, s, q, group):
                dve.wait_ge(s_up, s + 1)
                if later(s, 2):
                    dve.wait_ge(s_hid, s - 1)
                v.tensor_tensor(up_w[:, k % 2, :], ps[:, 2 * (k % 2) + 1, :],
                                route_w[:, group, 512 * q:512 * q + 512],
                                ALU.mult).then_inc(s_upw, 1)

            def hidden_lo(k, s):
                dve.wait_ge(s_hhi, s + 1)
                if later(s, 2):
                    dve.wait_ge(s_down, s - 1)
                v.tensor_tensor(hid_lo[:, k % 2, :], hid[:, k % 2, :], hid_hi[:, k % 2, :],
                                ALU.subtract).then_inc(s_hlo, 1)

            dve.wait_ge(s_shhi, 2 * SHARED)
            for c in range(SHARED):
                v.tensor_tensor(sh_lo[:, c, 0:2 * SROWS], sh_raw[:, c, 0:2 * SROWS],
                                sh_hi[:, c, 0:2 * SROWS], ALU.subtract).then_inc(s_shlo, 1)
                v.tensor_tensor(sh_lo[0:SROWS, c, WD:WD + P], sh_raw[0:SROWS, c, WD:WD + P],
                                sh_hi[0:SROWS, c, WD:WD + P], ALU.subtract).then_inc(s_shlo, 1)
            for c in range(AHEAD):
                split_lo(c, c, 16)
            dve.wait_ge(s_rw, SETS * QUADS)
            for s in range(STEPS0):
                dve.wait_ge(s_up, s + 1)
                if s >= 2:
                    dve.wait_ge(s_hid, s - 1)
                v.tensor_copy(up_w[0:SROWS, s % 2, :],
                              ps[0:SROWS, 2 * (s % 2) + 1, :]).then_inc(s_upw, 1)
                if s >= 1:
                    hidden_lo(s - 1, s - 1)

            def round_steps(r, last=False):
                for k in range(PER_ROUND):
                    s = r * PER_ROUND + (STEPS0 + k)
                    weigh(k, s, k % 4, k // 4)
                    hidden_lo(k - 1, s - 1)
                    c = k // 4 + AHEAD
                    if k % 4 == 1 and not (last and c >= SETS):
                        split_lo(c % SETS, r * SETS + c, (r + (1 + c // SETS)) * 16)

            with dve.Fori(0, ROUNDS - 1) as r:
                round_steps(r)
            round_steps(ROUNDS - 1, last=True)
            hidden_lo(ALL_STEPS - 1, ALL_STEPS - 1)

            for q in range(QUADS):
                own = slice(4 * q, 4 * q + 4)
                dve.wait_ge(s_yp, q + 1)
                statistics(lambda t: ps[:, q, P * t:P * t + P])
                dve.wait_ge(s_rstd, norms_done[0])
                for t in range(4):
                    ins = v.tensor_scalar(x_sb[:, 4 * q + t, :], ps[:, q, P * t:P * t + P],
                                          mv[:, t, 0:1], rstd[:, t:t + 1], ALU.subtract, ALU.mult)
                link(ins)
                v.tensor_tensor(flat(x_sb[:, own, :]), flat(x_sb[:, own, :]),
                                flat(x1_sb[:, own, :]), ALU.add).then_inc(s_y, 1)

        @block.tensor
        def _(pe):
            t_ = nc.tensor

            def bank_free(at, kinds, last):
                st = stage_before(at, kinds)
                if st:
                    pe.wait_ge(last[st[0]], st[1] + 1)

            def turn_xn(q, at):
                bank_free(at, "PE", {"P": s_xn_t, "E": s_xhi})
                pe.wait_ge(s_scaled, norm_of("P", q) + 1)
                for t in range(4):
                    mm = t_.transpose(ps[:, 0, P * t:P * t + P], xn[:, q % 2, t, :], ident[:])
                mm.then_inc(s_xn_tp, 1)

            def bank67_free(at, h):
                before = [st for st in ORDER[:at] if st[0] == "QV"[h] or (st[0] == "C" and st[2] == h)]
                if before:
                    what, q, _ = before[-1]
                    if what == "C":
                        pe.wait_ge(s_att, 2 * q + h + 1)
                    else:
                        pe.wait_ge(s_vt if h == 0 else s_v, q + 1)

            def bank1_free(at):
                bank_free(at, "QME", {"Q": s_llo, "M": s_mlo, "E": s_sc})

            def latent(q, at):
                pe.wait_ge(s_xn_t, q + 1)
                bank1_free(at)
                t_.matmul(ps[:, 1, :], wb_sb[:], xn_t[:, q % 2, :], start=True,
                          stop=True).then_inc(s_lat, 1)
                bank67_free(at, 0)
                t_.matmul(ps[:, 6, :], wv_sb[:], xn_t[:, q % 2, :], start=True,
                          stop=True).then_inc(s_vtp, 1)

            def values(q, at):
                pe.wait_ge(s_vt, q + 1)
                bank67_free(at, 1)
                for t in range(4):
                    mm = t_.matmul(ps[:, 7, P * t:P * t + P], v_t[:, q % 2, P * t:P * t + P],
                                   wo_sb[:], start=True, stop=True)
                mm.then_inc(s_vp, 1)

            def score_rows(q, r):
                base = (q // QPB) * seq
                i = keys_of(q) - 4 + r
                free = 4 * q + r - (1 if q % QPB == 0 and r else 0)
                if free:
                    pe.wait_ge(s_max, free)
                pe.wait_ge(s_llo, q + 1)
                first = 2 + (r % 2 if q % QPB == 0 else 0)
                own = lat_hl[:, 512 * q + P * r:512 * q + P * r + P]
                for lo in range(0, P * i + P, 512):
                    w = min(512, P * i + P - lo)
                    keys = slice(base + lo, base + lo + w)
                    o = ps[:, first + lo // 512, :]
                    t_.matmul(o[:, 0:w], own, lat_hi[:, keys], start=True, stop=False)
                    mm = t_.matmul(o[:, 0:w], own, lat_lo[:, keys], start=False, stop=True)
                mm = t_.matmul(o[:, w - P:w], ident_r[:], mask_rows, start=False, stop=True,
                               skip_group_check=True)
                mm.then_inc(s_rows, 1)

            def max_row(q, at):
                bank1_free(at)
                pe.wait_ge(s_max, 4 * q + 4)
                for r in range(4):
                    mm = t_.matmul(ps[:, 1, P * r:P * r + P],
                                   neg_max[:, 4 * q + r:4 * q + r + 1].to_broadcast([P, P]),
                                   ident[:], start=True, stop=True)
                mm.then_inc(s_mrow, 1)

            def score_cols(q, j):
                base = (q // QPB) * seq
                n = cols_before(q) + j
                d = j - (keys_of(q) - 4)
                lo = P * max(d, 0)
                pe.wait_ge(s_mlo, q + 1)
                if n >= 2:
                    pe.wait_ge(s_exp, n - 1)
                o = ps[:, 4 + n % 2, lo:512]
                keys = lat_hl[:, base + P * j:base + P * j + P]
                cols = slice(512 * q + lo, 512 * q + 512)
                t_.matmul(o, keys, lat_hi[:, cols], start=True, stop=False)
                t_.matmul(o, keys, lat_lo[:, cols], start=False, stop=False)
                mm = t_.matmul(o, pick[:], neg_max_t[:, q % 2, lo:512], start=False, stop=True)
                if d >= 0:
                    mm = t_.matmul(ps[:, 4 + n % 2, lo:lo + P], ident_r[:], mask_cols,
                                   start=False, stop=True, skip_group_check=True)
                mm.then_inc(s_cols, 1)

            def weigh_values(q, h, at):
                pe.wait_ge(s_v, q + 1)
                pe.wait_ge(s_exp, cols_before(q) + keys_of(q))
                bank67_free(at, h)
                for r in (2 * h, 2 * h + 1):
                    i = keys_of(q) - 4 + r
                    for j in range(i + 1):
                        mm = t_.matmul(ps[:, 6 + h, 256 * (r % 2):256 * (r % 2) + C + 1],
                                       exp_t[:, q % 2, j, P * r:P * r + P],
                                       vals[:, (q // QPB) * TPB + j, 0:C + 1], start=(j == 0),
                                       stop=(j == i))
                mm.then_inc(s_pv, 1)

            def expert_input(q, at):
                bank_free(at, "PE", {"P": s_xn_t, "E": s_xhi})
                pe.wait_ge(s_scaled, norm_of("D", q) + 2)
                for t in range(4):
                    mm = t_.transpose(ps[:, 0, P * t:P * t + P], xn2[:, t, :], ident[:])
                mm.then_inc(s_x2p, 1)
                bank1_free(at)
                pe.wait_ge(s_x2, q + 1)
                for t in range(4):
                    mm = t_.matmul(ps[:, 1, E * t:E * t + E], x2_t[:, P * t:P * t + P], gw_sb[:],
                                   start=True, stop=True)
                mm.then_inc(s_lg, 1)

            def turn_route(q):
                pe.wait_ge(s_rx, q + 1)
                for g in range(SETS):
                    n = SETS * q + g
                    if n < 2:
                        pe.wait_ge(s_max, TILES)
                    else:
                        pe.wait_ge(s_rw, n - 1)
                    for t in range(4):
                        mm = t_.transpose(
                            ps[:, 2 + n % 2, P * t:P * t + P],
                            route_x[:, t, PER_CHUNK * g:PER_CHUNK * (g + 1), :]
                            .rearrange("p e k -> p (e k)"), ident[:])
                    mm.then_inc(s_rtp, 1)

            pe.wait_ge(s_const, 1)
            pe.wait_ge(s_w, 16 * W_LOADS)
            for at, (what, q, n) in enumerate(ORDER):
                if what == "P":
                    turn_xn(q, at)
                elif what == "Q":
                    latent(q, at)
                elif what == "V":
                    values(q, at)
                elif what == "A":
                    score_rows(q, n)
                elif what == "M":
                    max_row(q, at)
                elif what == "B":
                    score_cols(q, n)
                elif what == "C":
                    weigh_values(q, n, at)
                elif what == "E":
                    expert_input(q, at)
                elif what == "G":
                    turn_route(q)

            def products(out_, hi, lo, mhi, mlo, start, stop):
                t_.matmul(out_, hi, mhi, start=start, stop=False)
                t_.matmul(out_, hi, mlo, start=False, stop=False)
                return t_.matmul(out_, lo, mhi, start=False, stop=stop)

            def gate_up(k, s, q, whi, wlo, n):
                cols = slice(512 * q, 512 * q + 512)
                if later(s, 2):
                    pe.wait_ge(s_gated, s - 1)
                products(ps[0:n, 2 * (k % 2), :], whi[:, 0:n], wlo[:, 0:n], x_hi[:, cols],
                         x_lo[:, cols], True, True).then_inc(s_gate, 1)
                if later(s, 2):
                    pe.wait_ge(s_upw, s - 1)
                products(ps[0:n, 2 * (k % 2) + 1, :], whi[:, n:2 * n], wlo[:, n:2 * n],
                         x_hi[:, cols], x_lo[:, cols], True, True).then_inc(s_up, 1)

            def down(k, s, q, whi, wlo, n, start=False, stop=False):
                pe.wait_ge(s_hlo, s + 1)
                products(ps[:, 4 + q, :], whi[0:n, WD:WD + P], wlo[0:n, WD:WD + P],
                         hid_hi[0:n, k % 2, :], hid_lo[0:n, k % 2, :], start,
                         stop).then_inc(s_down, 1)

            def shared_down(s):
                c = s // 4
                down(s, s, s % 4, sh_hi[:, c, :], sh_lo[:, c, :], SROWS, start=(c == 0))

            pe.wait_ge(s_shlo, 2 * SHARED)
            pe.wait_ge(s_xlo, QUADS)
            pe.wait_ge(s_rw, SETS * QUADS)
            pe.wait_ge(s_sc, QUADS)
            pe.wait_ge(s_att, 2 * QUADS)
            for s in range(STEPS0):
                c = s // 4
                gate_up(s, s, s % 4, sh_hi[:, c, :], sh_lo[:, c, :], SROWS)
                if s >= LAG:
                    shared_down(s - LAG)

            def round_steps(r, first=False, last=False):
                for k in range(PER_ROUND):
                    s = r * PER_ROUND + (STEPS0 + k)
                    c = k // 4
                    if k % 4 == 0:
                        pe.wait_ge(s_wlo, r * SETS + (c + 1))
                    gate_up(k, s, k % 4, w_hi[:, c, :], w_lo[:, c, :], P)
                    if first and k < LAG:
                        shared_down(s - LAG)
                    else:
                        kd = (k - LAG) % PER_ROUND
                        down(kd, s - LAG, kd % 4, w_hi[:, kd // 4, :], w_lo[:, kd // 4, :], P,
                             stop=(last and k - LAG >= PER_ROUND - 4))

            round_steps(0, first=True)
            with pe.Fori(1, ROUNDS - 1) as r:
                round_steps(r)
            round_steps(ROUNDS - 1, last=True)
            for k in range(PER_ROUND - LAG, PER_ROUND):
                down(k, ALL_STEPS - PER_ROUND + k, k % 4, w_hi[:, k // 4, :], w_lo[:, k // 4, :],
                     P, stop=True)
            for q in range(QUADS):
                pe.wait_ge(s_yt, q + 1)
                if q == 0:
                    pe.wait_ge(s_gated, ALL_STEPS)
                    pe.wait_ge(s_upw, ALL_STEPS)
                for t in range(4):
                    mm = t_.transpose(ps[:, q, P * t:P * t + P], y_t[:, q, P * t:P * t + P],
                                      ident[:])
                mm.then_inc(s_yp, 1)




def kernel(L0_attn_hidden_states, L0_attn_W_basis, L0_attn_W_v, L0_attn_b_v, L0_attn_W_o,
           L0_attn_b_o, L0_ffn_gate_w, L0_ffn_gate_bias, L0_ffn_Wg, L0_ffn_Wu, L0_ffn_Wd,
           L0_ffn_Sg, L0_ffn_Su, L0_ffn_Sd):
    import concourse.bacc as bacc
    from concourse.bass_utils import run_bass_kernel_spmd

    E, I, H = L0_ffn_Wg.shape
    sets, rounds = E // PER_CHUNK, I // PACK
    up = [np.asarray(w).reshape(sets, PER_CHUNK, rounds, PACK, H).transpose(2, 0, 4, 1, 3)
          .reshape(rounds, sets, H, P) for w in (L0_ffn_Wg, L0_ffn_Wu)]
    down = (np.asarray(L0_ffn_Wd).reshape(sets, PER_CHUNK, H, rounds, PACK)
            .transpose(3, 0, 1, 4, 2).reshape(rounds, sets, P, H))
    shared = 2
    s_up = [np.asarray(w).reshape(shared, -1, H).transpose(0, 2, 1) for w in (L0_ffn_Sg, L0_ffn_Su)]
    arrays = {
        "x": np.asarray(L0_attn_hidden_states),
        "w_basis_t": np.asarray(L0_attn_W_basis).T,
        "w_v_t": np.asarray(L0_attn_W_v).T,
        "b_v": np.asarray(L0_attn_b_v)[:, None],
        "w_o_t": np.asarray(L0_attn_W_o).T,
        "b_o": np.asarray(L0_attn_b_o)[None, :],
        "gate_w_t": np.asarray(L0_ffn_gate_w).T,
        "gate_bias": np.asarray(L0_ffn_gate_bias)[None, :],
        "w_experts": np.concatenate([*up, down], axis=3),
        "w_shared_up": np.concatenate(s_up, axis=2),
        "w_shared_down": np.asarray(L0_ffn_Sd).T.reshape(shared, -1, H),
    }
    arrays = {k: np.ascontiguousarray(a) for k, a in arrays.items()}
    nc = bacc.Bacc("TRN2", target_bir_lowering=False, num_devices=1)
    args = [nc.dram_tensor(f"in_{k}", a.shape, F32, kind="ExternalInput").ap()
            for k, a in arrays.items()]
    out = nc.dram_tensor("out", arrays["x"].shape, F32, kind="ExternalOutput").ap()
    build(nc, *args, out)
    r = run_bass_kernel_spmd(nc, [{f"in_{k}": a for k, a in arrays.items()}], core_ids=[0])
    return r.results[0]["out"]
```

```python
from contextlib import ExitStack

import numpy as np

import concourse.bass as bass
from concourse import mybir

F32 = mybir.dt.float32
F32R = mybir.dt.float32r
ACT = mybir.ActivationFunctionType
ALU = mybir.AluOpType
AX = mybir.AxisListType

P = 128
EXPERTS = 64
GROUPS = 8
TOP_GROUPS = 4
ROUTED_SCALE = 2.5
EPS = 1e-5
MASKED = -1e30
TAKEN = -3e38
NO_SCORE = 3e38
PACK = 8
PER_CHUNK = P // PACK


def build(nc, x, w_basis_t, w_v, b_v, w_o_t, b_o, gate_w_t, gate_bias, w_experts, w_shared_up,
          w_shared_down, out):
    batches, seq, C = x.shape
    R = w_basis_t.shape[1]
    TILES = batches * seq // P
    QUADS = TILES // 4
    QPB = seq // 512
    TPB = seq // P
    ROUNDS, SETS = w_experts.shape[0], w_experts.shape[1]
    SHARED, _, TWO_S = w_shared_up.shape
    SROWS = TWO_S // 2
    SCALE = 1.0 / float(R) ** 0.5
    E = EXPERTS
    GE = E // GROUPS
    assert C == P and QPB == 2 and SETS * PER_CHUNK == E and QUADS == 4

    x_tiles = x.rearrange("b (t p) c -> p (b t) c", p=P)
    out_tiles = out.rearrange("b (t p) c -> p (b t) c", p=P)

    with ExitStack() as ctx:
        def sb(name, shape, dt=F32):
            return ctx.enter_context(nc.sbuf_tensor(name, shape, dt))

        def sem(name):
            return ctx.enter_context(nc.semaphore(name))

        ps = ctx.enter_context(nc.psum_tensor("ps", [P, 8, 512], F32))

        ident = sb("ident", [P, P])
        ident_r = sb("ident_r", [P, P], F32R)
        mask_f = sb("mask_f", [P, 2, P])
        masks = sb("masks", [P, 2, P], F32R)
        mask_rows = masks[:, 0, :]
        mask_cols = masks[:, 1, :]
        pick_f = sb("pick_f", [P, P])
        pick = sb("pick", [P, P], F32R)
        wb_sb = sb("wb_sb", [P, 2 * R])
        wv_sb = sb("wv_sb", [P, P])
        wo_sb = sb("wo_sb", [P, P])
        gw_sb = sb("gw_sb", [P, E])
        bv_sb = sb("bv_sb", [P, 1])
        bo_sb = sb("bo_sb", [P, P])
        gb_sb = sb("gb_sb", [P, E])
        x_sb = sb("x_sb", [P, TILES, C])
        x1_sb = sb("x1_sb", [P, TILES, C])
        stats = sb("stats", [P, 4, 6])
        mv = sb("mv", [P, 4, 4, 2])
        rstd = sb("rstd", [P, 4, 4])
        var_e = sb("var_e", [P, 4])
        minus_half = sb("minus_half", [P, 4])
        xn = sb("xn", [P, 2, 4, C])
        xn_t = sb("xn_t", [P, 2, 512])
        lat_hi = sb("lat_hi", [P, TILES * P], F32R)
        lat_lo = sb("lat_lo", [P, TILES * P], F32R)
        lat_hl = sb("lat_hl", [P, TILES * P], F32R)
        neg_max_t = sb("neg_max_t", [P, 2, 512], F32R)
        wvo_sb = sb("wvo_sb", [P, C])
        vals = sb("vals", [P, TILES, C + 4])
        neg_max = sb("neg_max", [P, TILES])
        arena = sb("arena", [P, 2 * TPB * 512])
        exp_t = arena[:, :].rearrange("p (k j n) -> p k j n", k=2, j=TPB)
        half = TPB * 512
        y_t = arena[:, half:half + 512 * QUADS].rearrange("p (q n) -> p q n", n=512)
        half += 512 * QUADS
        gated = arena[:, half:half + 1024].rearrange("p (k n) -> p k n", k=2)
        up_w = arena[:, half + 1024:half + 2048].rearrange("p (k n) -> p k n", k=2)
        row_sum_inv = sb("row_sum_inv", [P, TILES])
        att = sb("att", [P, 2, 4, C])
        xn2 = sb("xn2", [P, 4, C])
        x2_t = sb("x2_t", [P, 512])
        x_hi = sb("x_hi", [P, TILES * P], F32R)
        x_lo = sb("x_lo", [P, TILES * P], F32R)
        scores = sb("scores", [P, 2, 4, E])
        choice = sb("choice", [P, 4, E])
        big = [sb(f"big{n}", [P, 4 * GROUPS, 4 >> n]) for n in range(3)]
        small = [sb(f"small{n}", [P, 4 * GROUPS, 4 >> n]) for n in range(3)]
        low_big = sb("low_big", [P, 4 * GROUPS, 2])
        group_score = sb("group_score", [P, 4, GROUPS])
        group_top = sb("group_top", [P, 4, 8])
        group_find = sb("group_find", [P, 4, 8])
        group_left = sb("group_left", [P, 4, GROUPS])
        group_in = sb("group_in", [P, 4, GROUPS])
        masked = sb("masked", [P, 4, E])
        top8 = sb("top8", [P, 4, 8])
        left = sb("left", [P, 4, E])
        route = sb("route", [P, 4, E])
        route_x = sb("route_x", [P, 4, E, PACK])
        wsum = sb("wsum", [P, 4])
        winv = sb("winv", [P, 4])
        route_w = sb("route_w", [P, SETS, TILES * P])
        sh_raw = sb("sh_raw", [P, SHARED, 3 * P])
        sh_hi = sb("sh_hi", [P, SHARED, 3 * P], F32R)
        sh_lo = sb("sh_lo", [P, SHARED, 3 * P], F32R)
        w_raw = sb("w_raw", [P, SETS, 3 * P])
        w_hi = sb("w_hi", [P, SETS, 3 * P], F32R)
        w_lo = sb("w_lo", [P, SETS, 3 * P], F32R)
        hid = arena[:, 0:1024].rearrange("p (k n) -> p k n", k=2)
        hid_hi = lat_hl[:, 0:1024].rearrange("p (k n) -> p k n", k=2)
        hid_lo = lat_hl[:, 1024:2048].rearrange("p (k n) -> p k n", k=2)

        s_x = [sem(f"x_loaded{q}") for q in range(QUADS)]
        s_w = sem("small_weights_loaded")
        s_const = sem("constants_made")
        s_pool = sem("pool_step")
        s_dve = sem("dve_step")
        s_act = sem("act_step")
        s_var = sem("variance_ready")
        s_rstd = sem("rstd_ready")
        s_xn = sem("xn_ready")
        s_xn_tp = sem("xn_transposed_psum")
        s_xn_t = sem("xn_t_ready")
        s_lat = sem("latent_psum")
        s_lhi = sem("lat_hi_ready")
        s_llo = sem("lat_lo_ready")
        s_wvop = sem("wvo_psum")
        s_wvo = sem("wvo_ready")
        s_vp = sem("vals_psum")
        s_v = sem("vals_ready")
        s_rows = sem("score_rows_psum")
        s_max = sem("row_max_ready")
        s_mrow = sem("max_row_psum")
        s_mhi = sem("neg_max_hi_ready")
        s_mlo = sem("neg_max_t_ready")
        s_cols = sem("score_cols_psum")
        s_exp = sem("exp_ready")
        s_pv = sem("att_psum")
        s_att = sem("att_ready")
        s_xn2 = sem("xn2_ready")
        s_x2p = sem("x2_t_psum")
        s_x2 = sem("x2_t_ready")
        s_xhi = sem("x_hi_ready")
        s_xlo = sem("x_lo_ready")
        s_lg = sem("logits_psum")
        s_sc = sem("scores_ready")
        s_route = sem("route_ready")
        s_rx = sem("route_x_ready")
        s_rtp = sem("route_t_psum")
        s_rw = sem("route_w_ready")
        s_wl = [sem(f"expert_w_loaded{k}") for k in range(SETS)]
        s_shl = sem("shared_w_loaded")
        s_shhi = sem("shared_hi_ready")
        s_shlo = sem("shared_lo_ready")
        s_whi = sem("w_hi_ready")
        s_wlo = sem("w_lo_ready")
        s_gate = sem("gate_psum")
        s_up = sem("up_psum")
        s_gated = sem("gated_ready")
        s_upw = sem("up_weighted")
        s_hid = sem("hidden_ready")
        s_hhi = sem("hidden_hi_ready")
        s_hlo = sem("hidden_lo_ready")
        s_down = sem("down_done")
        s_yt = sem("y_t_ready")
        s_yp = sem("y_psum")
        s_y = sem("y_ready")
        s_out = sem("out_stored")

        W_LOADS = 8
        ORDER = [(n[0], int(n[1]), int(n[2:] or 0)) for n in (
            "S0 P0 Q0 S1 P1 S2 A00 Q1 A01 A02 A03 V0 A10 M0 B00 P2 B01 V1 S3 A11 B02 A12 B03 P3 "
            "A13 Q2 V2 Q3 C00 C01 A20 M1 B10 B11 B12 D0 B13 V3 A21 B14 B15 A22 B16 B17 A23 C10 X0 "
            "A30 M2 C11 Y0 B20 B21 D1 E0 A31 B22 B23 A32 C20 A33 C21 F0 H0 M3 B30 X1 B31 D2 B32 "
            "B33 B34 B35 B36 B37 Y1 X2 I0 C30 E1 F1 Y2 K0 H1 I1 C31 D3 E2 X3 G0 K1 F2 Y3 L0 G1 L1 "
            "H2 Z0 I2 Z1 E3 F3 W0 K2 H3 Z2 W1 Z3 W2 G2 I3 Z4 W3 K3 Z5 W4 Z6 R0 G3 W5 W6 Z7 R1 "
        ).split()]

        def keys_of(q):
            return 4 * (q % QPB) + 4

        def cols_before(q):
            return sum(keys_of(k) for k in range(q))

        def stage_before(at, kinds):
            found = [st for st in ORDER[:at] if st[0] in kinds]
            return found[-1] if found else None

        NORMS = [st[:2] for st in ORDER if st[0] in "SDX"]

        def buffer_of(what, q):
            return q % 2 + (0 if what == "S" else 2)

        STEPS0 = QUADS * SHARED
        PER_ROUND = 4 * SETS
        ALL_STEPS = STEPS0 + ROUNDS * PER_ROUND
        LAG = 2
        AHEAD = 2
        WD = 2 * P

        def gate_bank(k):
            return 4 if k % 2 == 0 else 2

        Y_OUT = 4 + LAG
        Y_TURN = Y_OUT + 1
        Y_STATS = Y_OUT + 2
        Y_NORM = Y_OUT + 3

        def quads_at(k, stage):
            return [q for q in range(QUADS) if k == 4 * q + stage]

        LAST_S = ALL_STEPS - PER_ROUND
        TAIL = range(4 * QUADS + Y_NORM)

        def acc_bank(q):
            return (6, 7, 0, 1)[q]

        def later(s, n):
            return not isinstance(s, int) or s >= n

        block = ctx.enter_context(nc.Block())

        @block.sync
        def _(sp):
            sp.dma_start(x_sb[:, 0:4, :], x_tiles[:, 0:4, :]).then_inc(s_x[0], 16)
            for half in range(2):
                sp.dma_start(wb_sb[:, R * half:R * half + R], w_basis_t).then_inc(s_w, 16)
            sp.dma_start(wv_sb[:], w_v).then_inc(s_w, 16)
            sp.dma_start(wo_sb[:], w_o_t).then_inc(s_w, 16)
            sp.dma_start(bv_sb[:], b_v).then_inc(s_w, 16)
            sp.dma_start(bo_sb[:], b_o.to_broadcast([P, C])).then_inc(s_w, 16)
            sp.dma_start(gw_sb[:], gate_w_t).then_inc(s_w, 16)
            sp.dma_start(gb_sb[:], gate_bias.to_broadcast([P, E])).then_inc(s_w, 16)
            for q in range(1, QUADS):
                sp.dma_start(x_sb[:, 4 * q:4 * q + 4, :],
                             x_tiles[:, 4 * q:4 * q + 4, :]).then_inc(s_x[q], 16)
            for c in range(SHARED):
                sp.dma_start(sh_raw[:, c, 0:2 * SROWS], w_shared_up[c]).then_inc(s_shl, 16)
                sp.dma_start(sh_raw[0:SROWS, c, WD:WD + P], w_shared_down[c]).then_inc(s_shl, 16)
            for c in range(SETS):
                sp.dma_start(w_raw[:, c, :], w_experts[0, c]).then_inc(s_wl[c], 16)
            with sp.Fori(0, ROUNDS - 1) as r:
                for c in range(SETS):
                    sp.wait_ge(s_whi, r * SETS + (c + 1))
                    sp.wait_ge(s_wlo, r * SETS + (c + 1))
                    sp.dma_start(w_raw[:, c, :], w_experts[r + 1, c]).then_inc(s_wl[c], 16)
            for q in range(QUADS):
                sp.wait_ge(s_y, q + 1)
                sp.dma_start(out_tiles[:, 4 * q:4 * q + 4, :],
                             x_sb[:, 4 * q:4 * q + 4, :]).then_inc(s_out, 16)
            sp.wait_ge(s_out, 16 * QUADS)

        @block.gpsimd
        def _(pool):
            g = nc.gpsimd
            steps = [0]

            def link(ins):
                steps[0] += 1
                ins.then_inc(s_pool, 1)
                pool.wait_ge(s_pool, steps[0])

            g.memset(ident[:], 0.0)
            g.memset(minus_half[:], -0.5)
            g.memset(mask_f[:], 0.0)
            g.memset(pick_f[:], 0.0)
            g.memset(group_find[:], NO_SCORE)
            link(g.memset(vals[:, :, C:C + 4], 1.0))
            link(g.memset(pick_f[0:1, :], 1.0))
            link(g.memset(pick_f[R:R + 1, :], 1.0))
            g.affine_select(out=ident[:], in_=ident[:], compare_op=ALU.not_equal, fill=1.0, base=0,
                            pattern=[[-1, P]], channel_multiplier=1)
            g.affine_select(out=mask_f[:, 0, :], in_=mask_f[:, 0, :], compare_op=ALU.is_ge,
                            fill=MASKED, base=0, pattern=[[-1, P]], channel_multiplier=1)
            link(g.affine_select(out=mask_f[:, 1, :], in_=mask_f[:, 1, :], compare_op=ALU.is_ge,
                            fill=MASKED, base=0, pattern=[[1, P]], channel_multiplier=-1))
            g.tensor_copy(ident_r[:], ident[:])
            g.tensor_copy(pick[:], pick_f[:])
            g.tensor_copy(masks[:], mask_f[:]).then_inc(s_const, 1)

            def low_part(q):
                pool.wait_ge(s_x2, q + 1)
                pool.wait_ge(s_xhi, q + 1)
                g.tensor_tensor(x_lo[:, 512 * q:512 * q + 512], x2_t[:, :], x_hi[:, 512 * q:512 * q + 512],
                                ALU.subtract).then_inc(s_xlo, 1)

            def inv_sqrt(n, k):
                if n:
                    pool.wait_ge(s_rstd, n)
                pool.wait_ge(s_var, n + 1)
                link(g.tensor_scalar(var_e[:], mv[:, k, :, 1], EPS, None, ALU.add))
                g.tensor_tensor(rstd[:, k], var_e[:], minus_half[:], ALU.pow).then_inc(s_rstd, 1)

            def hidden(k, s, rows=P):
                pool.wait_ge(s_gated, s + 1)
                pool.wait_ge(s_upw, s + 1)
                if later(s, 2):
                    pool.wait_ge(s_hlo, s - 1)
                g.tensor_tensor(hid[0:rows, k, :], gated[0:rows, k, :], up_w[0:rows, k, :],
                                ALU.mult).then_inc(s_hid, 1)

            for what, q, _ in ORDER:
                if what in "SDX":
                    inv_sqrt(NORMS.index((what, q)), buffer_of(what, q))
                elif what == "E":
                    low_part(q)
                elif what == "Z":
                    if q == 0:
                        pool.wait_ge(s_pv, 2 * QUADS)
                        link(g.memset(hid, 0.0))
                    hidden(q % 2, q, SROWS)
            with pool.Fori(0, ROUNDS - 1) as r:
                for k in range(PER_ROUND):
                    hidden(k % 2, r * PER_ROUND + (STEPS0 + k))
            for k in TAIL:
                if k < PER_ROUND:
                    hidden(k % 2, LAST_S + k)
                for q in quads_at(k, Y_STATS):
                    inv_sqrt(len(NORMS) + q, 2 + q % 2)

        @block.scalar
        def _(act):
            a = nc.scalar

            def keep_xn_t(q):
                act.wait_ge(s_xn_tp, q + 1)
                if q >= 2:
                    act.wait_ge(s_lat, q - 1)
                    act.wait_ge(s_vp, q - 1)
                a.copy(xn_t[:, q % 2, :], ps[:, 0, :]).then_inc(s_xn_t, 1)

            def keep_latent(q):
                own = slice(512 * q, 512 * q + 512)
                act.wait_ge(s_lat, q + 1)
                a.copy(lat_hi[:, own], ps[:, 1, :])
                a.copy(lat_hl[0:R, own], ps[0:R, 1, :]).then_inc(s_lhi, 1)

            def keep_values(q):
                act.wait_ge(s_vp, q + 1)
                a.copy(vals[:, 4 * q:4 * q + 4, 0:C],
                       ps[:, 7, :].rearrange("p (t c) -> p t c", t=4)).then_inc(s_v, 1)

            def max_row(q):
                act.wait_ge(s_mrow, q + 1)
                if q >= 2:
                    act.wait_ge(s_cols, cols_before(q - 1))
                a.copy(neg_max_t[:, q % 2, :], ps[:, 1, :]).then_inc(s_mhi, 1)

            def exp_cols(q, j):
                d = j - (keys_of(q) - 4)
                act.wait_ge(s_cols, cols_before(q) + j + 1)
                if q >= 2 and j == 0:
                    act.wait_ge(s_pv, 2 * q - 2)
                lo = P * max(d, 0)
                a.activation(exp_t[:, q % 2, j, lo:512],
                             ps[:, 4 + (cols_before(q) + j) % 2, lo:512], ACT.Exp,
                             scale=SCALE).then_inc(s_exp, 1)

            def expert_input(q):
                act.wait_ge(s_x2p, q + 1)
                if q >= 1:
                    act.wait_ge(s_lg, q)
                    act.wait_ge(s_xlo, q)
                a.copy(x2_t[:, :], ps[:, 0, :]).then_inc(s_x2, 1)
                a.copy(x_hi[:, 512 * q:512 * q + 512], ps[:, 0, :]).then_inc(s_xhi, 1)

            def keep_logits(q):
                act.wait_ge(s_lg, q + 1)
                if q >= 2:
                    act.wait_ge(s_route, q - 1)
                a.activation(scores[:, q % 2].rearrange("p t e -> p (t e)"), ps[:, 1, 0:4 * E],
                             ACT.Sigmoid).then_inc(s_sc, 1)

            def repeat_route(q):
                act.wait_ge(s_route, q + 1)
                if q >= 1:
                    act.wait_ge(s_rtp, SETS * q)
                a.copy(route_x[:], route[:, :, :].unsqueeze(3).to_broadcast([P, 4, E, PACK])
                       ).then_inc(s_rx, 1)

            def keep_route(q):
                for g in range(SETS):
                    n = SETS * q + g
                    act.wait_ge(s_rtp, n + 1)
                    a.copy(route_w[:, g, 512 * q:512 * q + 512],
                           ps[:, 2 + n % 2, :]).then_inc(s_rw, 1)

            def split_hi(c, n, loads):
                act.wait_ge(s_wl[c], loads)
                if later(n, SETS):
                    act.wait_ge(s_down, (n - (SETS - 1)) * 4 + STEPS0)
                a.copy(w_hi[:, c, :], w_raw[:, c, :]).then_inc(s_whi, 1)

            def gate(k, s, rows=P, bank=None):
                act.wait_ge(s_gate, s + 1)
                if later(s, 2):
                    act.wait_ge(s_hid, s - 1)
                a.activation(gated[0:rows, k % 2, :], ps[0:rows, gate_bank(k) if bank is None else bank, :],
                             ACT.Silu).then_inc(s_gated, 1)

            def hidden_hi(k, s):
                act.wait_ge(s_hid, s + 1)
                if later(s, 2):
                    act.wait_ge(s_down, s - 1)
                a.copy(hid_hi[:, k % 2, :], hid[:, k % 2, :]).then_inc(s_hhi, 1)

            act.wait_ge(s_wvop, 1)
            a.copy(wvo_sb[:], ps[:, 7, 0:C]).then_inc(s_wvo, 1)
            for what, q, n in ORDER:
                if what == "P":
                    keep_xn_t(q)
                elif what == "Q":
                    keep_latent(q)
                elif what == "V":
                    keep_values(q)
                elif what == "M":
                    max_row(q)
                elif what == "B":
                    exp_cols(q, n)
                elif what == "E":
                    expert_input(q)
                elif what == "K":
                    repeat_route(q)
                elif what == "G":
                    keep_route(q)
                elif what == "F":
                    keep_logits(q)
                elif what == "L":
                    act.wait_ge(s_shl, 16 * 2 * SHARED)
                    a.copy(sh_hi[:, q, 0:2 * SROWS],
                           sh_raw[:, q, 0:2 * SROWS]).then_inc(s_shhi, 1)
                    a.copy(sh_hi[0:SROWS, q, WD:WD + P],
                           sh_raw[0:SROWS, q, WD:WD + P]).then_inc(s_shhi, 1)
                elif what == "R":
                    split_hi(q, q, 16)
                elif what == "Z":
                    gate(q, q, SROWS, gate_bank(0))
                elif what == "W":
                    hidden_hi(q, q)

            with act.Fori(0, ROUNDS - 1) as r:
                for k in range(PER_ROUND):
                    s = r * PER_ROUND + (STEPS0 + k)
                    gate(k, s)
                    hidden_hi(k - 1, s - 1)
                    c = k // 4 + AHEAD
                    if k % 4 == 1:
                        split_hi(c % SETS, r * SETS + c, (r + (1 + c // SETS)) * 16)
            for k in TAIL:
                if k < PER_ROUND:
                    gate(k, LAST_S + k)
                if k <= PER_ROUND:
                    hidden_hi(k - 1, LAST_S + k - 1)
                c = k + AHEAD
                if c < SETS:
                    split_hi(c, (ROUNDS - 1) * SETS + c, ROUNDS * 16)
                for q in quads_at(k, Y_OUT):
                    act.wait_ge(s_down, LAST_S + 4 * q + 4)
                    a.copy(y_t[:, q, :], ps[:, acc_bank(q), :]).then_inc(s_yt, 1)

        @block.vector
        def _(dve):
            v = nc.vector
            steps = [0]

            def link(ins):
                steps[0] += 1
                ins.then_inc(s_dve, 1)
                dve.wait_ge(s_dve, steps[0])

            def statistics(k, src):
                if made[0]:
                    dve.wait_ge(s_var, made[0])
                made[0] += 1
                for t in range(4):
                    ins = v.bn_stats(stats[:, t, :], src(t))
                link(ins)
                for t in range(4):
                    ins = v.bn_aggr(mv[:, k, t, :], stats[:, t, :])
                ins.then_inc(s_var, 1)

            made = [0]

            def scale(n, k, src, dst):
                dve.wait_ge(s_rstd, n + 1)
                for t in range(4):
                    ins = v.tensor_scalar(dst(t), src(t), mv[:, k, t, 0:1], rstd[:, k, t:t + 1],
                                          ALU.subtract, ALU.mult)
                return ins

            def flat(t3):
                return t3.rearrange("p a b -> p (a b)")

            def latent_lo(q):
                own = slice(512 * q, 512 * q + 512)
                dve.wait_ge(s_lhi, q + 1)
                link(v.tensor_tensor(lat_lo[:, own], ps[:, 1, :], lat_hi[:, own], ALU.subtract))
                v.tensor_copy(lat_hl[R:2 * R, own], lat_lo[R:2 * R, own]).then_inc(s_llo, 1)

            def row_max(q, r):
                i = keys_of(q) - 4 + r
                first = 2 + (r % 2 if q % QPB == 0 else 0)
                rows = ps[:, first:4, :].rearrange("p a b -> p (a b)")
                dve.wait_ge(s_rows, 4 * q + r + 1)
                v.tensor_reduce(neg_max[:, 4 * q + r:4 * q + r + 1], rows[:, 0:P * i + P],
                                AX.X, ALU.max, negate=True).then_inc(s_max, 1)

            def max_row_lo(q):
                dve.wait_ge(s_mhi, q + 1)
                low = neg_max_t[R:P, q % 2, :]
                v.tensor_tensor(low, ps[R:P, 1, :], low, ALU.subtract).then_inc(s_mlo, 1)

            def divide(q, h):
                dve.wait_ge(s_pv, 2 * q + h + 1)
                bank = ps[:, 6 + h, :].rearrange("p (t c) -> p t c", t=2)
                inv = row_sum_inv[:, 4 * q + 2 * h:4 * q + 2 * h + 2]
                link(v.reciprocal(inv, bank[:, :, C]))
                for t in range(2):
                    ins = v.scalar_tensor_tensor(
                        out=att[:, q % 2, 2 * h + t, :], in0=bank[:, t, 0:C],
                        scalar=inv[:, t:t + 1], in1=bo_sb[:], op0=ALU.mult, op1=ALU.add)
                ins.then_inc(s_att, 1)

            def norm_x(q):
                if q >= 2:
                    dve.wait_ge(s_xn_tp, q - 1)
                scale(NORMS.index(("S", q)), q % 2, lambda t: x_sb[:, 4 * q + t, :],
                      lambda t: xn[:, q % 2, t, :]).then_inc(s_xn, 1)

            def add_attention(q):
                own = slice(4 * q, 4 * q + 4)
                link(scale(NORMS.index(("D", q)), 2 + q % 2, lambda t: att[:, q % 2, t, :],
                           lambda t: x1_sb[:, 4 * q + t, :]))
                link(v.tensor_tensor(x1_sb[:, own, :], x1_sb[:, own, :], x_sb[:, own, :],
                                     ALU.add))
                statistics(2 + q % 2, lambda t: x1_sb[:, 4 * q + t, :])

            def norm_x1(q):
                if q >= 1:
                    dve.wait_ge(s_x2p, q)
                scale(NORMS.index(("X", q)), 2 + q % 2, lambda t: x1_sb[:, 4 * q + t, :],
                      lambda t: xn2[:, t, :]).then_inc(s_xn2, 1)

            tt = v.tensor_tensor

            def choose_groups(q):
                k = q % 2
                dve.wait_ge(s_sc, q + 1)
                link(tt(choice[:], scores[:, k], gb_sb[:, :].unsqueeze(1).to_broadcast([P, 4, E]),
                        ALU.add))
                grp = choice[:, :, :].rearrange("p t (g k) -> p (t g) k", k=GE)
                tt(big[0][:], grp[:, :, 0:4], grp[:, :, 4:8], ALU.max)
                link(tt(small[0][:], grp[:, :, 0:4], grp[:, :, 4:8], ALU.min))
                for n in range(2):
                    w = 2 >> n
                    b0, b1 = big[n][:, :, 0:w], big[n][:, :, w:2 * w]
                    tt(big[n + 1][:], b0, b1, ALU.max)
                    tt(low_big[:, :, 0:w], b0, b1, ALU.min)
                    link(tt(small[n + 1][:], small[n][:, :, 0:w], small[n][:, :, w:2 * w],
                            ALU.max))
                    link(tt(small[n + 1][:], small[n + 1][:], low_big[:, :, 0:w], ALU.max))
                link(tt(group_score[:, :, :].rearrange("p t g -> p (t g)"), big[2][:, :, 0],
                        small[2][:, :, 0], ALU.add))
                for t in range(4):
                    ins = v.max(group_top[:, t, :], group_score[:, t, :])
                link(ins)
                link(v.tensor_copy(group_find[:, :, 0:TOP_GROUPS], group_top[:, :, 0:TOP_GROUPS]))
                for t in range(4):
                    ins = v.match_replace(group_left[:, t, :], group_find[:, t, :],
                                          group_score[:, t, :], TAKEN)
                link(ins)
                link(tt(group_in[:], group_left[:], group_score[:], ALU.not_equal))
                link(tt(masked[:].rearrange("p t (g k) -> p t g k", k=GE),
                   choice[:, :, :].rearrange("p t (g k) -> p t g k", k=GE),
                   group_in[:, :, :].unsqueeze(3).to_broadcast([P, 4, GROUPS, GE]),
                   ALU.mult))

            def choose_experts(q):
                k = q % 2
                for t in range(4):
                    ins = v.max(top8[:, t, :], masked[:, t, :])
                link(ins)
                for t in range(4):
                    ins = v.match_replace(left[:, t, :], top8[:, t, :], masked[:, t, :], TAKEN)
                link(ins)
                link(v.tensor_tensor(left[:], left[:], masked[:], ALU.not_equal))
                link(v.tensor_tensor(left[:], left[:], scores[:, k], ALU.mult))
                link(v.tensor_reduce(wsum[:], left[:], AX.X, ALU.add))
                link(v.tensor_scalar(wsum[:], wsum[:], 1e-20, 1.0 / ROUTED_SCALE, ALU.add, ALU.mult))
                link(v.reciprocal(winv[:], wsum[:]))
                if q >= 1:
                    dve.wait_ge(s_rx, q)
                v.tensor_tensor(route[:], left[:],
                                winv[:, :].unsqueeze(2).to_broadcast([P, 4, E]),
                                ALU.mult).then_inc(s_route, 1)

            def split_lo(c, n, loads):
                dve.wait_ge(s_wl[c], loads)
                dve.wait_ge(s_whi, n + 1)
                if later(n, SETS):
                    dve.wait_ge(s_down, (n - (SETS - 1)) * 4 + STEPS0)
                v.tensor_tensor(w_lo[:, c, :], w_raw[:, c, :], w_hi[:, c, :],
                                ALU.subtract).then_inc(s_wlo, 1)

            def weigh(k, s, q, group):
                dve.wait_ge(s_up, s + 1)
                if later(s, 2):
                    dve.wait_ge(s_hid, s - 1)
                v.tensor_tensor(up_w[:, k % 2, :], ps[:, gate_bank(k) + 1, :],
                                route_w[:, group, 512 * q:512 * q + 512],
                                ALU.mult).then_inc(s_upw, 1)

            def hidden_lo(k, s):
                dve.wait_ge(s_hhi, s + 1)
                if later(s, 2):
                    dve.wait_ge(s_down, s - 1)
                v.tensor_tensor(hid_lo[:, k % 2, :], hid[:, k % 2, :], hid_hi[:, k % 2, :],
                                ALU.subtract).then_inc(s_hlo, 1)

            for at, (what, q, n) in enumerate(ORDER):
                if at == 1:
                    dve.wait_ge(s_wvop, 2)
                    link(tt(bo_sb[:], bo_sb[:], ps[:, 6, 0:C], ALU.add))
                if what == "S":
                    dve.wait_ge(s_x[q], 16)
                    if q >= 2:
                        dve.wait_ge(s_xn, q - 1)
                    statistics(q % 2, lambda t: x_sb[:, 4 * q + t, :])
                elif what == "P":
                    norm_x(q)
                elif what == "Q":
                    latent_lo(q)
                elif what == "A":
                    row_max(q, n)
                elif what == "M":
                    max_row_lo(q)
                elif what == "C":
                    divide(q, n)
                elif what == "D":
                    dve.wait_ge(s_att, 2 * q + 2)
                    if q >= 2:
                        dve.wait_ge(s_xn2, q - 1)
                    statistics(2 + q % 2, lambda t: att[:, q % 2, t, :])
                elif what == "X":
                    add_attention(q)
                elif what == "Y":
                    norm_x1(q)
                elif what == "H":
                    choose_groups(q)
                elif what == "I":
                    choose_experts(q)
                elif what == "L":
                    dve.wait_ge(s_shhi, 2 * q + 2)
                    v.tensor_tensor(sh_lo[:, q, 0:2 * SROWS], sh_raw[:, q, 0:2 * SROWS],
                                    sh_hi[:, q, 0:2 * SROWS], ALU.subtract).then_inc(s_shlo, 1)
                    v.tensor_tensor(sh_lo[0:SROWS, q, WD:WD + P],
                                    sh_raw[0:SROWS, q, WD:WD + P],
                                    sh_hi[0:SROWS, q, WD:WD + P],
                                    ALU.subtract).then_inc(s_shlo, 1)
                elif what == "R":
                    split_lo(q, q, 16)
                elif what == "Z":
                    dve.wait_ge(s_up, q + 1)
                    if q >= 2:
                        dve.wait_ge(s_hid, q - 1)
                    v.tensor_copy(up_w[0:SROWS, q % 2, :],
                                  ps[0:SROWS, gate_bank(0) + 1, :]).then_inc(s_upw, 1)
                elif what == "W":
                    hidden_lo(q, q)

            dve.wait_ge(s_rw, SETS * QUADS)

            with dve.Fori(0, ROUNDS - 1) as r:
                for k in range(PER_ROUND):
                    s = r * PER_ROUND + (STEPS0 + k)
                    weigh(k, s, k % 4, k // 4)
                    hidden_lo(k - 1, s - 1)
                    c = k // 4 + AHEAD
                    if k % 4 == 1:
                        split_lo(c % SETS, r * SETS + c, (r + (1 + c // SETS)) * 16)

            for k in TAIL:
                if k < PER_ROUND:
                    weigh(k, LAST_S + k, k // 4, k % 4)
                if k <= PER_ROUND:
                    hidden_lo(k - 1, LAST_S + k - 1)
                c = k + AHEAD
                if c < SETS:
                    split_lo(c, (ROUNDS - 1) * SETS + c, ROUNDS * 16)
                for q in quads_at(k, Y_STATS):
                    dve.wait_ge(s_yp, q + 1)
                    dve.wait_ge(s_xn2, QUADS)
                    statistics(2 + q % 2, lambda t: ps[:, acc_bank(q), P * t:P * t + P])
                for q in quads_at(k, Y_NORM):
                    own = slice(4 * q, 4 * q + 4)
                    link(scale(len(NORMS) + q, 2 + q % 2,
                               lambda t: ps[:, acc_bank(q), P * t:P * t + P],
                               lambda t: x_sb[:, 4 * q + t, :]))
                    v.tensor_tensor(flat(x_sb[:, own, :]), flat(x_sb[:, own, :]),
                                    flat(x1_sb[:, own, :]), ALU.add).then_inc(s_y, 1)

        @block.tensor
        def _(pe):
            t_ = nc.tensor

            def bank_free(at, kinds, last):
                st = stage_before(at, kinds)
                if st:
                    pe.wait_ge(last[st[0]], st[1] + 1)

            def turn_xn(q, at):
                bank_free(at, "PE", {"P": s_xn_t, "E": s_xhi})
                pe.wait_ge(s_xn, q + 1)
                for t in range(4):
                    mm = t_.transpose(ps[:, 0, P * t:P * t + P], xn[:, q % 2, t, :], ident[:])
                mm.then_inc(s_xn_tp, 1)

            def bank67_free(at, h):
                before = [st for st in ORDER[:at]
                          if (st[0] == "V" and h == 1) or (st[0] == "C" and st[2] == h)]
                if before:
                    what, q, _ = before[-1]
                    if what == "C":
                        pe.wait_ge(s_att, 2 * q + h + 1)
                    else:
                        pe.wait_ge(s_v, q + 1)

            def bank1_free(at):
                bank_free(at, "QMF", {"Q": s_llo, "M": s_mlo, "F": s_sc})

            def banks23_free(at, rows=None):
                st = stage_before(at, "AG")
                if st and st[0] == "A":
                    done = 4 * st[1] + st[2] + 1
                    if rows and rows[0] % QPB == 0 and rows[1] > 0:
                        done -= 1
                    if done:
                        pe.wait_ge(s_max, done)
                elif st:
                    pe.wait_ge(s_rw, SETS * (st[1] + 1))

            def latent(q, at):
                pe.wait_ge(s_xn_t, q + 1)
                bank1_free(at)
                t_.matmul(ps[:, 1, :], wb_sb[:], xn_t[:, q % 2, :], start=True,
                          stop=True).then_inc(s_lat, 1)

            def values(q, at):
                pe.wait_ge(s_xn_t, q + 1)
                pe.wait_ge(s_wvo, 1)
                bank67_free(at, 1)
                for t in range(4):
                    mm = t_.matmul(ps[:, 7, P * t:P * t + P], xn_t[:, q % 2, P * t:P * t + P],
                                   wvo_sb[:], start=True, stop=True)
                mm.then_inc(s_vp, 1)

            def score_rows(q, r, at):
                base = (q // QPB) * seq
                i = keys_of(q) - 4 + r
                banks23_free(at, (q, r))
                pe.wait_ge(s_llo, q + 1)
                first = 2 + (r % 2 if q % QPB == 0 else 0)
                own = lat_hl[:, 512 * q + P * r:512 * q + P * r + P]
                for lo in range(0, P * i + P, 512):
                    w = min(512, P * i + P - lo)
                    keys = slice(base + lo, base + lo + w)
                    o = ps[:, first + lo // 512, :]
                    t_.matmul(o[:, 0:w], own, lat_hi[:, keys], start=True, stop=False)
                    mm = t_.matmul(o[:, 0:w], own, lat_lo[:, keys], start=False, stop=True)
                mm = t_.matmul(o[:, w - P:w], ident_r[:], mask_rows, start=False, stop=True,
                               skip_group_check=True)
                mm.then_inc(s_rows, 1)

            def max_row(q, at):
                bank1_free(at)
                pe.wait_ge(s_max, 4 * q + 4)
                for r in range(4):
                    mm = t_.matmul(ps[:, 1, P * r:P * r + P],
                                   neg_max[:, 4 * q + r:4 * q + r + 1].to_broadcast([P, P]),
                                   ident[:], start=True, stop=True)
                mm.then_inc(s_mrow, 1)

            def score_cols(q, j):
                base = (q // QPB) * seq
                n = cols_before(q) + j
                d = j - (keys_of(q) - 4)
                lo = P * max(d, 0)
                pe.wait_ge(s_mlo, q + 1)
                if n >= 2:
                    pe.wait_ge(s_exp, n - 1)
                o = ps[:, 4 + n % 2, lo:512]
                keys = lat_hl[:, base + P * j:base + P * j + P]
                cols = slice(512 * q + lo, 512 * q + 512)
                t_.matmul(o, keys, lat_hi[:, cols], start=True, stop=False)
                t_.matmul(o, keys, lat_lo[:, cols], start=False, stop=False)
                mm = t_.matmul(o, pick[:], neg_max_t[:, q % 2, lo:512], start=False, stop=True)
                if d >= 0:
                    mm = t_.matmul(ps[:, 4 + n % 2, lo:lo + P], ident_r[:], mask_cols,
                                   start=False, stop=True, skip_group_check=True)
                mm.then_inc(s_cols, 1)

            def weigh_values(q, h, at):
                pe.wait_ge(s_v, q + 1)
                pe.wait_ge(s_exp, cols_before(q) + keys_of(q))
                bank67_free(at, h)
                for r in (2 * h, 2 * h + 1):
                    i = keys_of(q) - 4 + r
                    for j in range(i + 1):
                        mm = t_.matmul(ps[:, 6 + h, 256 * (r % 2):256 * (r % 2) + C + 1],
                                       exp_t[:, q % 2, j, P * r:P * r + P],
                                       vals[:, (q // QPB) * TPB + j, 0:C + 1], start=(j == 0),
                                       stop=(j == i))
                mm.then_inc(s_pv, 1)

            def expert_input(q, at):
                bank_free(at, "PE", {"P": s_xn_t, "E": s_xhi})
                pe.wait_ge(s_xn2, q + 1)
                for t in range(4):
                    mm = t_.transpose(ps[:, 0, P * t:P * t + P], xn2[:, t, :], ident[:])
                mm.then_inc(s_x2p, 1)

            def logits(q, at):
                bank1_free(at)
                pe.wait_ge(s_x2, q + 1)
                for t in range(4):
                    mm = t_.matmul(ps[:, 1, E * t:E * t + E], x2_t[:, P * t:P * t + P], gw_sb[:],
                                   start=True, stop=True)
                mm.then_inc(s_lg, 1)

            def turn_route(q, at):
                pe.wait_ge(s_rx, q + 1)
                for g in range(SETS):
                    n = SETS * q + g
                    if g == 0:
                        banks23_free(at)
                    elif g >= 2:
                        pe.wait_ge(s_rw, n - 1)
                    for t in range(4):
                        mm = t_.transpose(
                            ps[:, 2 + n % 2, P * t:P * t + P],
                            route_x[:, t, PER_CHUNK * g:PER_CHUNK * (g + 1), :]
                            .rearrange("p e k -> p (e k)"), ident[:])
                    mm.then_inc(s_rtp, 1)

            def products(out_, hi, lo, mhi, mlo, start, stop):
                t_.matmul(out_, hi, mhi, start=start, stop=False)
                t_.matmul(out_, hi, mlo, start=False, stop=False)
                return t_.matmul(out_, lo, mhi, start=False, stop=stop)

            def gate_up(k, s, q, whi, wlo, n, same=False):
                g, used = gate_bank(k), 0 if same else 1
                cols = slice(512 * q, 512 * q + 512)
                if later(s, 1 + used):
                    pe.wait_ge(s_gated, s - used)
                products(ps[0:n, g, :], whi[:, 0:n], wlo[:, 0:n], x_hi[:, cols],
                         x_lo[:, cols], True, True).then_inc(s_gate, 1)
                if later(s, 1 + used):
                    pe.wait_ge(s_upw, s - used)
                products(ps[0:n, g + 1, :], whi[:, n:2 * n], wlo[:, n:2 * n],
                         x_hi[:, cols], x_lo[:, cols], True, True).then_inc(s_up, 1)

            def down(k, s, q, whi, wlo, n, start=False, stop=False):
                pe.wait_ge(s_hlo, s + 1)
                products(ps[:, acc_bank(q), :], whi[0:n, WD:WD + P], wlo[0:n, WD:WD + P],
                         hid_hi[0:n, k % 2, :], hid_lo[0:n, k % 2, :], start,
                         stop).then_inc(s_down, 1)

            def shared_gate_up(s, at):
                c = s % SHARED
                if s == 0:
                    pe.wait_ge(s_exp, cols_before(QUADS))
                    pe.wait_ge(s_shlo, 2 * SHARED)
                pe.wait_ge(s_xlo, s // SHARED + 1)
                gate_up(0, s, s // SHARED, sh_hi[:, c, :], sh_lo[:, c, :], SROWS, same=True)

            def shared_down(s):
                q, c = s // SHARED, s % SHARED
                if c == 0:
                    if q < 2:
                        pe.wait_ge(s_att, 2 * QUADS)
                    elif q == 2:
                        pe.wait_ge(s_xhi, QUADS)
                    else:
                        pe.wait_ge(s_sc, QUADS)
                down(s, s, q, sh_hi[:, c, :], sh_lo[:, c, :], SROWS, start=(c == 0))

            pe.wait_ge(s_w, 16 * W_LOADS)
            t_.matmul(ps[:, 7, 0:C], wv_sb[:], wo_sb[:], start=True, stop=True).then_inc(s_wvop, 1)
            t_.matmul(ps[:, 6, 0:C], bv_sb[:, 0:1].to_broadcast([P, P]), wo_sb[:], start=True,
                      stop=True).then_inc(s_wvop, 1)
            pe.wait_ge(s_const, 1)
            for at, (what, q, n) in enumerate(ORDER):
                if what == "P":
                    turn_xn(q, at)
                elif what == "Q":
                    latent(q, at)
                elif what == "V":
                    values(q, at)
                elif what == "A":
                    score_rows(q, n, at)
                elif what == "M":
                    max_row(q, at)
                elif what == "B":
                    score_cols(q, n)
                elif what == "C":
                    weigh_values(q, n, at)
                elif what == "E":
                    expert_input(q, at)
                elif what == "G":
                    turn_route(q, at)
                elif what == "F":
                    logits(q, at)
                elif what == "Z":
                    shared_gate_up(q, at)
                elif what == "W":
                    shared_down(q)

            pe.wait_ge(s_rw, SETS * QUADS)

            def round_steps(r, first=False):
                for k in range(PER_ROUND):
                    s = r * PER_ROUND + (STEPS0 + k)
                    c = k // 4
                    if k % 4 == 0:
                        pe.wait_ge(s_wlo, r * SETS + (c + 1))
                    gate_up(k, s, k % 4, w_hi[:, c, :], w_lo[:, c, :], P,
                            same=(first and k == 0))
                    if first and k < LAG:
                        if k == LAG - 1:
                            shared_down(STEPS0 - 1)
                    else:
                        kd = (k - LAG) % PER_ROUND
                        down(kd, s - LAG, kd % 4, w_hi[:, kd // 4, :], w_lo[:, kd // 4, :], P)

            round_steps(0, first=True)
            with pe.Fori(1, ROUNDS - 1) as r:
                round_steps(r)
            for k in TAIL:
                if k < PER_ROUND:
                    c = k % 4
                    if k < SETS:
                        pe.wait_ge(s_wlo, (ROUNDS - 1) * SETS + c + 1)
                    gate_up(k, LAST_S + k, k // 4, w_hi[:, c, :], w_lo[:, c, :], P)
                kd = k - LAG
                if kd < 0:
                    down(kd, LAST_S + kd, kd % 4, w_hi[:, SETS - 1, :], w_lo[:, SETS - 1, :], P)
                elif kd < PER_ROUND:
                    c = kd % 4
                    down(kd, LAST_S + kd, kd // 4, w_hi[:, c, :], w_lo[:, c, :], P,
                         stop=(c == SETS - 1))
                for q in quads_at(k, Y_TURN):
                    pe.wait_ge(s_yt, q + 1)
                    for t in range(4):
                        mm = t_.transpose(ps[:, acc_bank(q), P * t:P * t + P],
                                          y_t[:, q, P * t:P * t + P], ident[:])
                    mm.then_inc(s_yp, 1)




def kernel(L0_attn_hidden_states, L0_attn_W_basis, L0_attn_W_v, L0_attn_b_v, L0_attn_W_o,
           L0_attn_b_o, L0_ffn_gate_w, L0_ffn_gate_bias, L0_ffn_Wg, L0_ffn_Wu, L0_ffn_Wd,
           L0_ffn_Sg, L0_ffn_Su, L0_ffn_Sd):
    import concourse.bacc as bacc
    from concourse.bass_utils import run_bass_kernel_spmd

    E, I, H = L0_ffn_Wg.shape
    sets, rounds = E // PER_CHUNK, I // PACK
    up = [np.asarray(w).reshape(sets, PER_CHUNK, rounds, PACK, H).transpose(2, 0, 4, 1, 3)
          .reshape(rounds, sets, H, P) for w in (L0_ffn_Wg, L0_ffn_Wu)]
    down = (np.asarray(L0_ffn_Wd).reshape(sets, PER_CHUNK, H, rounds, PACK)
            .transpose(3, 0, 1, 4, 2).reshape(rounds, sets, P, H))
    shared = 2
    s_up = [np.asarray(w).reshape(shared, -1, H).transpose(0, 2, 1) for w in (L0_ffn_Sg, L0_ffn_Su)]
    arrays = {
        "x": np.asarray(L0_attn_hidden_states),
        "w_basis_t": np.asarray(L0_attn_W_basis).T,
        "w_v": np.asarray(L0_attn_W_v),
        "b_v": np.asarray(L0_attn_b_v)[:, None],
        "w_o_t": np.asarray(L0_attn_W_o).T,
        "b_o": np.asarray(L0_attn_b_o)[None, :],
        "gate_w_t": np.asarray(L0_ffn_gate_w).T,
        "gate_bias": np.asarray(L0_ffn_gate_bias)[None, :],
        "w_experts": np.concatenate([*up, down], axis=3),
        "w_shared_up": np.concatenate(s_up, axis=2),
        "w_shared_down": np.asarray(L0_ffn_Sd).T.reshape(shared, -1, H),
    }
    arrays = {k: np.ascontiguousarray(a) for k, a in arrays.items()}
    nc = bacc.Bacc("TRN2", target_bir_lowering=False, num_devices=1)
    args = [nc.dram_tensor(f"in_{k}", a.shape, F32, kind="ExternalInput").ap()
            for k, a in arrays.items()]
    out = nc.dram_tensor("out", arrays["x"].shape, F32, kind="ExternalOutput").ap()
    build(nc, *args, out)
    r = run_bass_kernel_spmd(nc, [{f"in_{k}": a for k, a in arrays.items()}], core_ids=[0])
    return r.results[0]["out"]
```

```python
from contextlib import ExitStack

import numpy as np

import concourse.bass as bass
from concourse import mybir

F32 = mybir.dt.float32
F32R = mybir.dt.float32r
ACT = mybir.ActivationFunctionType
ALU = mybir.AluOpType
AX = mybir.AxisListType

P = 128
EXPERTS = 64
GROUPS = 8
TOP_GROUPS = 4
ROUTED_SCALE = 2.5
EPS = 1e-5
MASKED = -1e30
TAKEN = -3e38
NO_SCORE = 3e38
PACK = 8
PER_CHUNK = P // PACK


def build(nc, x, w_basis_t, w_v, b_v, w_o_t, b_o, gate_w_t, gate_bias, w_experts, w_shared_up,
          w_shared_down, out):
    batches, seq, C = x.shape
    R = w_basis_t.shape[1]
    TILES = batches * seq // P
    QUADS = TILES // 4
    QPB = seq // 512
    TPB = seq // P
    ROUNDS, SETS = w_experts.shape[0], w_experts.shape[1]
    SHARED, _, TWO_S = w_shared_up.shape
    SROWS = TWO_S // 2
    SCALE = 1.0 / float(R) ** 0.5
    E = EXPERTS
    GE = E // GROUPS
    assert C == P and QPB == 2 and SETS * PER_CHUNK == E and QUADS == 4

    x_tiles = x.rearrange("b (t p) c -> p (b t) c", p=P)
    out_tiles = out.rearrange("b (t p) c -> p (b t) c", p=P)

    with ExitStack() as ctx:
        def sb(name, shape, dt=F32):
            return ctx.enter_context(nc.sbuf_tensor(name, shape, dt))

        def sem(name):
            return ctx.enter_context(nc.semaphore(name))

        ps = ctx.enter_context(nc.psum_tensor("ps", [P, 8, 512], F32))

        ident = sb("ident", [P, P])
        ident_r = sb("ident_r", [P, P], F32R)
        mask_f = sb("mask_f", [P, 2, P])
        masks = sb("masks", [P, 2, P], F32R)
        mask_rows = masks[:, 0, :]
        mask_cols = masks[:, 1, :]
        pick_f = sb("pick_f", [P, P])
        pick = sb("pick", [P, P], F32R)
        wb_sb = sb("wb_sb", [P, 2 * R])
        wv_sb = sb("wv_sb", [P, P])
        wo_sb = sb("wo_sb", [P, P])
        gw_sb = sb("gw_sb", [P, E])
        bv_sb = sb("bv_sb", [P, 1])
        bo_sb = sb("bo_sb", [P, P])
        gb_sb = sb("gb_sb", [P, E])
        x_sb = sb("x_sb", [P, TILES, C])
        x1_sb = sb("x1_sb", [P, TILES, C])
        stats = sb("stats", [P, 4, 6])
        mv = sb("mv", [P, 4, 4, 2])
        rstd = sb("rstd", [P, 4, 4])
        var_e = sb("var_e", [P, 4])
        minus_half = sb("minus_half", [P, 4])
        xn = sb("xn", [P, 2, 4, C])
        xn_t = sb("xn_t", [P, 2, 512])
        lat_hi = sb("lat_hi", [P, TILES * P], F32R)
        lat_lo = sb("lat_lo", [P, TILES * P], F32R)
        lat_hl = sb("lat_hl", [P, TILES * P], F32R)
        neg_max_t = sb("neg_max_t", [P, 2, 512], F32R)
        wvo_sb = sb("wvo_sb", [P, C])
        vals = sb("vals", [P, TILES, C + 4])
        neg_max = sb("neg_max", [P, TILES])
        arena = sb("arena", [P, 2 * TPB * 512])
        exp_t = arena[:, :].rearrange("p (k j n) -> p k j n", k=2, j=TPB)
        hid, gated, up_w = (arena[:, n:n + 1024].rearrange("p (k n) -> p k n", k=2)
                            for n in (0, 1024, 2048))
        half = TPB * 512
        y_t = arena[:, half:half + 512 * QUADS].rearrange("p (q n) -> p q n", n=512)
        row_sum_inv = sb("row_sum_inv", [P, TILES])
        att = sb("att", [P, 2, 4, C])
        xn2 = sb("xn2", [P, 4, C])
        x2_t = sb("x2_t", [P, 512])
        x_hi = sb("x_hi", [P, TILES * P], F32R)
        x_lo = sb("x_lo", [P, TILES * P], F32R)
        scores = sb("scores", [P, 2, 4, E])
        choice = sb("choice", [P, 2, 4, E])
        big = [sb(f"big{n}", [P, 4 * GROUPS, 4 >> n]) for n in range(3)]
        small = [sb(f"small{n}", [P, 4 * GROUPS, 4 >> n]) for n in range(3)]
        low_big = sb("low_big", [P, 4 * GROUPS, 2])
        group_score = sb("group_score", [P, 4, GROUPS])
        group_top = sb("group_top", [P, 4, 8])
        group_find = sb("group_find", [P, 4, 8])
        group_left = sb("group_left", [P, 4, GROUPS])
        group_in = sb("group_in", [P, 4, GROUPS])
        masked = sb("masked", [P, 4, E])
        top8 = sb("top8", [P, 4, 8])
        left = sb("left", [P, 4, E])
        route = sb("route", [P, 4, E])
        route_x = sb("route_x", [P, 4, E, PACK])
        wsum = sb("wsum", [P, 4])
        winv = sb("winv", [P, 4])
        route_w = sb("route_w", [P, SETS, TILES * P])
        sh_raw = sb("sh_raw", [P, SHARED, 3 * P])
        sh_hi = sb("sh_hi", [P, SHARED, 3 * P], F32R)
        sh_lo = sb("sh_lo", [P, SHARED, 3 * P], F32R)
        w_raw = sb("w_raw", [P, SETS, 3 * P])
        w_hi = sb("w_hi", [P, SETS, 3 * P], F32R)
        w_lo = sb("w_lo", [P, SETS, 3 * P], F32R)
        hid_hi = lat_hl[:, 0:1024].rearrange("p (k n) -> p k n", k=2)
        hid_lo = lat_hi[:, 0:1024].rearrange("p (k n) -> p k n", k=2)

        s_x = [sem(f"x_loaded{q}") for q in range(QUADS)]
        s_w = sem("small_weights_loaded")
        s_const = sem("constants_made")
        s_pool = sem("pool_step")
        s_dve = sem("dve_step")
        s_act = sem("act_step")
        s_var = sem("variance_ready")
        s_rstd = sem("rstd_ready")
        s_xn = sem("xn_ready")
        s_xn_tp = sem("xn_transposed_psum")
        s_xn_t = sem("xn_t_ready")
        s_lat = sem("latent_psum")
        s_lhi = sem("lat_hi_ready")
        s_llo = sem("lat_lo_ready")
        s_wvop = sem("wvo_psum")
        s_wvo = sem("wvo_ready")
        s_vp = sem("vals_psum")
        s_v = sem("vals_ready")
        s_rows = sem("score_rows_psum")
        s_max = sem("row_max_ready")
        s_mrow = sem("max_row_psum")
        s_mhi = sem("neg_max_hi_ready")
        s_mlo = sem("neg_max_t_ready")
        s_cols = sem("score_cols_psum")
        s_exp = sem("exp_ready")
        s_pv = sem("att_psum")
        s_att = sem("att_ready")
        s_xn2 = sem("xn2_ready")
        s_x2p = sem("x2_t_psum")
        s_x2 = sem("x2_t_ready")
        s_xhi = sem("x_hi_ready")
        s_xlo = sem("x_lo_ready")
        s_lg = sem("logits_psum")
        s_sc = sem("scores_ready")
        s_choice = sem("choice_ready")
        s_gin = sem("groups_chosen")
        s_masked = sem("masked_ready")
        s_route = sem("route_ready")
        s_rx = sem("route_x_ready")
        s_rtp = sem("route_t_psum")
        s_rw = sem("route_w_ready")
        s_wl = [sem(f"expert_w_loaded{k}") for k in range(SETS)]
        s_shl = sem("shared_w_loaded")
        s_shhi = sem("shared_hi_ready")
        s_shlo = sem("shared_lo_ready")
        s_whi = sem("w_hi_ready")
        s_wlo = sem("w_lo_ready")
        s_gate = sem("gate_psum")
        s_up = sem("up_psum")
        s_gated = sem("gated_ready")
        s_upw = sem("up_weighted")
        s_hid0 = sem("hidden_cleared")
        s_hid = sem("hidden_ready")
        s_hhi = sem("hidden_hi_ready")
        s_hlo = sem("hidden_lo_ready")
        s_down = sem("down_done")
        s_yt = sem("y_t_ready")
        s_yp = sem("y_psum")
        s_y = sem("y_ready")
        s_out = sem("out_stored")

        W_LOADS = 8
        def stage(name):
            if name[0] in "ABCGK":
                return name[0], int(name[1]), int(name[2])
            return name[0], int(name[1:]), 0

        ORDER = [stage(name) for name in (
            "S0 P0 S1 S2 Q0 P1 A00 A01 A02 Q1 A03 V0 A10 M0 P2 B00 S3 B01 A11 Q2 B02 B03 V1 A12 "
            "C00 A13 C01 M1 A20 P3 V2 B10 D0 Q3 B11 L0 V3 A21 B12 B13 A22 B14 B15 A23 B16 B17 X0 "
            "M2 C10 A30 C11 D1 B20 Y0 B21 A31 X1 A32 B22 B23 C20 L1 E0 A33 F0 C21 Y1 M3 H0 R0 R1 "
            "B30 B31 J0 B32 E1 B33 D2 B34 I0 B35 B36 B37 O0 K00 F1 X2 C30 H1 Z0 J1 C31 Y2 K01 D3 "
            "W0 G00 I1 G01 Z1 Z2 O1 R2 W1 R3 E2 F2 X3 W2 Z3 Y3 K10 Z4 K11 H2 W3 E3 F3 J2 Z5 I2 O2 "
            "W4 G10 G11 K20 H3 K21 J3 W5 G20 Z6 G21 I3 W6 Z7 O3 W7 Z8 Z9 W8 K30 Z10 W9 Z11 W10 "
            "Z12 W11 Z13 K31 W12 G30 Z14 W13 Z15 W14 G31 Z16 W15 Z17 W16 Z18 W17 Z19 W18 Z20 W19 "
            "Z21 W20 Z22 W21 R4 Z23 W22 R5 "
        ).split()]

        def keys_of(q):
            return 4 * (q % QPB) + 4

        def cols_before(q):
            return sum(keys_of(k) for k in range(q))

        def stage_before(at, kinds):
            found = [st for st in ORDER[:at] if st[0] in kinds]
            return found[-1] if found else None

        NORMS = [st[:2] for st in ORDER if st[0] in "SDX"]

        def buffer_of(what, q):
            return q % 2 + (0 if what == "S" else 2)

        FIRST = []
        for quads in ((0,), (1, 2), (3,)):
            FIRST += [(q, c, False) for q in quads for c in range(SHARED)]
            FIRST += [(q, c, True) for q in quads for c in range(SETS)]
        FIRST_STEPS = len(FIRST)
        SHARED_STEPS = QUADS * SHARED

        def weighted(s):
            if not isinstance(s, int) or s >= FIRST_STEPS:
                return s - (SHARED_STEPS - 1)
            return sum(routed for _, _, routed in FIRST[:s + 1])

        def is_routed(s):
            return not isinstance(s, int) or s >= FIRST_STEPS or FIRST[s][2]

        STEPS0 = SHARED_STEPS
        PER_ROUND = 4 * SETS
        ALL_STEPS = STEPS0 + ROUNDS * PER_ROUND
        LAG = 2
        AHEAD = 2
        WD = 2 * P

        def gate_bank(k):
            return 4 if k % 2 == 0 else 2

        Y_OUT = 4 + LAG
        Y_TURN = Y_OUT + 1
        Y_STATS = Y_OUT + 2
        Y_NORM = Y_OUT + 3

        def quads_at(k, stage):
            return [q for q in range(QUADS) if k == 4 * q + stage]

        LAST_S = ALL_STEPS - PER_ROUND
        TAIL = range(4 * QUADS + Y_NORM)

        def acc_bank(q):
            return (6, 7, 0, 1)[q]

        def last_user(c):
            return max(s for s in range(FIRST_STEPS) if FIRST[s][1:] == (c, True))

        def free_at(r, c):
            return (r - 1) * PER_ROUND + (STEPS0 + 4 * c + 6)

        def norm_on_pool(what, q):
            return (what == "P" and q >= 2) or (what == "Y" and q < 2)

        def later(s, n):
            return not isinstance(s, int) or s >= n

        block = ctx.enter_context(nc.Block())

        @block.sync
        def _(sp):
            sp.dma_start(x_sb[:, 0:4, :], x_tiles[:, 0:4, :]).then_inc(s_x[0], 16)
            for half in range(2):
                sp.dma_start(wb_sb[:, R * half:R * half + R], w_basis_t).then_inc(s_w, 16)
            sp.dma_start(wv_sb[:], w_v).then_inc(s_w, 16)
            sp.dma_start(wo_sb[:], w_o_t).then_inc(s_w, 16)
            sp.dma_start(bv_sb[:], b_v).then_inc(s_w, 16)
            sp.dma_start(bo_sb[:], b_o.to_broadcast([P, C])).then_inc(s_w, 16)
            sp.dma_start(gw_sb[:], gate_w_t).then_inc(s_w, 16)
            sp.dma_start(gb_sb[:], gate_bias.to_broadcast([P, E])).then_inc(s_w, 16)
            for q in range(1, QUADS):
                sp.dma_start(x_sb[:, 4 * q:4 * q + 4, :],
                             x_tiles[:, 4 * q:4 * q + 4, :]).then_inc(s_x[q], 16)
            for c in range(SHARED):
                sp.dma_start(sh_raw[:, c, 0:2 * SROWS], w_shared_up[c]).then_inc(s_shl, 16)
                sp.dma_start(sh_raw[0:SROWS, c, WD:WD + P], w_shared_down[c]).then_inc(s_shl, 16)
            for c in range(SETS):
                sp.dma_start(w_raw[:, c, :], w_experts[0, c]).then_inc(s_wl[c], 16)
            with sp.Fori(0, ROUNDS - 1) as r:
                for c in range(SETS):
                    sp.wait_ge(s_whi, r * SETS + (c + 1))
                    sp.wait_ge(s_wlo, r * SETS + (c + 1))
                    sp.dma_start(w_raw[:, c, :], w_experts[r + 1, c]).then_inc(s_wl[c], 16)
            for q in range(QUADS):
                sp.wait_ge(s_y, q + 1)
                sp.dma_start(out_tiles[:, 4 * q:4 * q + 4, :],
                             x_sb[:, 4 * q:4 * q + 4, :]).then_inc(s_out, 16)
            sp.wait_ge(s_out, 16 * QUADS)

        @block.gpsimd
        def _(pool):
            g = nc.gpsimd
            steps = [0]

            def link(ins):
                steps[0] += 1
                ins.then_inc(s_pool, 1)
                pool.wait_ge(s_pool, steps[0])

            g.memset(ident[:], 0.0)
            g.memset(minus_half[:], -0.5)
            g.memset(mask_f[:], 0.0)
            g.memset(pick_f[:], 0.0)
            g.memset(group_find[:], NO_SCORE)
            link(g.memset(vals[:, :, C:C + 4], 1.0))
            link(g.memset(pick_f[0:1, :], 1.0))
            link(g.memset(pick_f[R:R + 1, :], 1.0))
            g.affine_select(out=ident[:], in_=ident[:], compare_op=ALU.not_equal, fill=1.0, base=0,
                            pattern=[[-1, P]], channel_multiplier=1)
            g.affine_select(out=mask_f[:, 0, :], in_=mask_f[:, 0, :], compare_op=ALU.is_ge,
                            fill=MASKED, base=0, pattern=[[-1, P]], channel_multiplier=1)
            link(g.affine_select(out=mask_f[:, 1, :], in_=mask_f[:, 1, :], compare_op=ALU.is_ge,
                            fill=MASKED, base=0, pattern=[[1, P]], channel_multiplier=-1))
            g.tensor_copy(ident_r[:], ident[:])
            g.tensor_copy(pick[:], pick_f[:])
            g.tensor_copy(masks[:], mask_f[:]).then_inc(s_const, 1)

            def low_part(q):
                pool.wait_ge(s_x2, q + 1)
                pool.wait_ge(s_xhi, q + 1)
                own = slice(512 * q, 512 * q + 512)
                g.tensor_tensor(x_lo[:, own], x2_t[:, :], x_hi[:, own],
                                ALU.subtract).then_inc(s_xlo, 1)

            def inv_sqrt(n, k):
                if n:
                    pool.wait_ge(s_rstd, n)
                pool.wait_ge(s_var, n + 1)
                link(g.tensor_scalar(var_e[:], mv[:, k, :, 1], EPS, None, ALU.add))
                g.tensor_tensor(rstd[:, k], var_e[:], minus_half[:], ALU.pow).then_inc(s_rstd, 1)

            def hidden(k, s):
                pool.wait_ge(s_gated, s + 1)
                pool.wait_ge(s_upw, weighted(s))
                if not is_routed(s - 1):
                    pool.wait_ge(s_hid, s)
                pool.wait_ge(s_hlo, s - 1)
                g.tensor_tensor(hid[:, k, :], gated[:, k, :], up_w[:, k, :],
                                ALU.mult).then_inc(s_hid, 1)

            def scale(n, k, src, dst):
                pool.wait_ge(s_rstd, n + 1)
                for t in range(4):
                    ins = g.tensor_scalar(dst(t), src(t), mv[:, k, t, 0:1], rstd[:, k, t:t + 1],
                                          ALU.subtract, ALU.mult)
                return ins

            def add_bias(q):
                pool.wait_ge(s_sc, q + 1)
                pool.wait_ge(s_w, 16 * W_LOADS)
                if q >= 2:
                    pool.wait_ge(s_gin, q - 1)
                    pool.wait_ge(s_masked, q - 1)
                g.tensor_tensor(choice[:, q % 2], scores[:, q % 2],
                                gb_sb[:, :].unsqueeze(1).to_broadcast([P, 4, E]),
                                ALU.add).then_inc(s_choice, 1)

            def mask_groups(q):
                pool.wait_ge(s_gin, q + 1)
                if q:
                    pool.wait_ge(s_route, q)
                g.tensor_tensor(masked[:].rearrange("p t (g k) -> p t g k", k=GE),
                                choice[:, q % 2].rearrange("p t (g k) -> p t g k", k=GE),
                                group_in[:, :, :].unsqueeze(3).to_broadcast([P, 4, GROUPS, GE]),
                                ALU.mult).then_inc(s_masked, 1)

            for what, q, _ in ORDER:
                if what in "SDX":
                    inv_sqrt(NORMS.index((what, q)), buffer_of(what, q))
                elif what == "P" and norm_on_pool(what, q):
                    pool.wait_ge(s_xn_tp, q - 1)
                    pool.wait_ge(s_xn, q)
                    scale(NORMS.index(("S", q)), q % 2, lambda t: x_sb[:, 4 * q + t, :],
                          lambda t: xn[:, q % 2, t, :]).then_inc(s_xn, 1)
                elif what == "Y" and norm_on_pool(what, q):
                    if q >= 1:
                        pool.wait_ge(s_x2p, q)
                    scale(NORMS.index(("X", q)), 2 + q % 2, lambda t: x1_sb[:, 4 * q + t, :],
                          lambda t: xn2[:, t, :]).then_inc(s_xn2, 1)
                elif what == "F":
                    add_bias(q)
                elif what == "J":
                    mask_groups(q)
                elif what == "L":
                    pool.wait_ge(s_shhi, 2 * q + 2)
                    g.tensor_tensor(sh_lo[:, q, 0:2 * SROWS], sh_raw[:, q, 0:2 * SROWS],
                                    sh_hi[:, q, 0:2 * SROWS], ALU.subtract).then_inc(s_shlo, 1)
                    g.tensor_tensor(sh_lo[0:SROWS, q, WD:WD + P],
                                    sh_raw[0:SROWS, q, WD:WD + P],
                                    sh_hi[0:SROWS, q, WD:WD + P],
                                    ALU.subtract).then_inc(s_shlo, 1)
                elif what == "R" and q < SETS:
                    pool.wait_ge(s_whi, q + 1)
                    g.tensor_tensor(w_lo[:, q, :], w_raw[:, q, :], w_hi[:, q, :],
                                    ALU.subtract).then_inc(s_wlo, 1)
                elif what == "E":
                    low_part(q)
                elif what == "Z" and q == 0:
                    pool.wait_ge(s_pv, 2 * (QUADS - 1))
                    g.memset(hid, 0.0).then_inc(s_hid0, 1)
                elif what == "Z" and is_routed(q):
                    hidden(q % 2, q)
            with pool.Fori(1, ROUNDS - 1) as r:
                for k in range(PER_ROUND):
                    hidden(k % 2, r * PER_ROUND + (STEPS0 + k))
            for k in TAIL:
                if k < PER_ROUND:
                    hidden(k % 2, LAST_S + k)
                for q in quads_at(k, Y_STATS):
                    inv_sqrt(len(NORMS) + q, 2 + q % 2)

        @block.scalar
        def _(act):
            a = nc.scalar

            def keep_xn_t(q):
                act.wait_ge(s_xn_tp, q + 1)
                if q >= 2:
                    act.wait_ge(s_lat, q - 1)
                    act.wait_ge(s_vp, q - 1)
                a.copy(xn_t[:, q % 2, :], ps[:, 0, :]).then_inc(s_xn_t, 1)

            def keep_latent(q):
                own = slice(512 * q, 512 * q + 512)
                act.wait_ge(s_lat, q + 1)
                a.copy(lat_hi[:, own], ps[:, 1, :])
                a.copy(lat_hl[0:R, own], ps[0:R, 1, :]).then_inc(s_lhi, 1)

            def keep_values(q):
                act.wait_ge(s_vp, q + 1)
                a.copy(vals[:, 4 * q:4 * q + 4, 0:C],
                       ps[:, 7, :].rearrange("p (t c) -> p t c", t=4)).then_inc(s_v, 1)

            def max_row(q):
                act.wait_ge(s_mrow, q + 1)
                if q >= 2:
                    act.wait_ge(s_cols, cols_before(q - 1))
                a.copy(neg_max_t[:, q % 2, :], ps[:, 1, :]).then_inc(s_mhi, 1)

            def exp_cols(q, j):
                d = j - (keys_of(q) - 4)
                act.wait_ge(s_cols, cols_before(q) + j + 1)
                if q >= 2 and j == 0:
                    act.wait_ge(s_pv, 2 * q - 2)
                lo = P * max(d, 0)
                a.activation(exp_t[:, q % 2, j, lo:512],
                             ps[:, 4 + (cols_before(q) + j) % 2, lo:512], ACT.Exp,
                             scale=SCALE).then_inc(s_exp, 1)

            def expert_input(q):
                act.wait_ge(s_x2p, q + 1)
                if q >= 1:
                    act.wait_ge(s_lg, q)
                    act.wait_ge(s_xlo, q)
                a.copy(x2_t[:, :], ps[:, 0, :]).then_inc(s_x2, 1)
                a.copy(x_hi[:, 512 * q:512 * q + 512], ps[:, 0, :]).then_inc(s_xhi, 1)

            def keep_logits(q):
                act.wait_ge(s_lg, q + 1)
                if q >= 2:
                    act.wait_ge(s_route, q - 1)
                a.activation(scores[:, q % 2].rearrange("p t e -> p (t e)"), ps[:, 1, 0:4 * E],
                             ACT.Sigmoid).then_inc(s_sc, 1)

            def repeat_route(q, h):
                act.wait_ge(s_route, q + 1)
                if q >= 1:
                    act.wait_ge(s_rtp, SETS * (q - 1) + 2 * h + 2)
                own = slice(E // 2 * h, E // 2 * h + E // 2)
                a.copy(route_x[:, :, own, :],
                       route[:, :, own].unsqueeze(3).to_broadcast([P, 4, E // 2, PACK])
                       ).then_inc(s_rx, 1)

            def keep_route(q, h):
                for g in (2 * h, 2 * h + 1):
                    n = SETS * q + g
                    act.wait_ge(s_rtp, n + 1)
                    a.copy(route_w[:, g, 512 * q:512 * q + 512],
                           ps[:, 2 + n % 2, :]).then_inc(s_rw, 1)

            def split_hi(c, loads, used):
                act.wait_ge(s_wl[c], 16 * loads)
                if used is not None:
                    act.wait_ge(s_down, used + 1)
                a.copy(w_hi[:, c, :], w_raw[:, c, :]).then_inc(s_whi, 1)

            def gate(k, s, rows=P):
                act.wait_ge(s_gate, s + 1)
                if later(s, 2):
                    act.wait_ge(s_hid, s - 1)
                a.activation(gated[0:rows, k % 2, :], ps[0:rows, gate_bank(k), :],
                             ACT.Silu).then_inc(s_gated, 1)

            def hidden_hi(k, s):
                act.wait_ge(s_hid, s + 1)
                if later(s, 2):
                    act.wait_ge(s_down, s - 1)
                a.copy(hid_hi[:, k % 2, :], hid[:, k % 2, :]).then_inc(s_hhi, 1)

            act.wait_ge(s_wvop, 1)
            a.copy(wvo_sb[:], ps[:, 7, 0:C]).then_inc(s_wvo, 1)
            for what, q, n in ORDER:
                if what == "P":
                    keep_xn_t(q)
                elif what == "Q":
                    keep_latent(q)
                elif what == "V":
                    keep_values(q)
                elif what == "M":
                    max_row(q)
                elif what == "B":
                    exp_cols(q, n)
                elif what == "E":
                    expert_input(q)
                elif what == "K":
                    repeat_route(q, n)
                elif what == "G":
                    keep_route(q, n)
                elif what == "F":
                    keep_logits(q)
                elif what == "L":
                    act.wait_ge(s_shl, 16 * 2 * SHARED)
                    a.copy(sh_hi[:, q, 0:2 * SROWS],
                           sh_raw[:, q, 0:2 * SROWS]).then_inc(s_shhi, 1)
                    a.copy(sh_hi[0:SROWS, q, WD:WD + P],
                           sh_raw[0:SROWS, q, WD:WD + P]).then_inc(s_shhi, 1)
                elif what == "R":
                    split_hi(q % SETS, q // SETS + 1, last_user(q - SETS) if q >= SETS else None)
                elif what == "Z":
                    gate(q, q, P if is_routed(q) else SROWS)
                elif what == "W":
                    hidden_hi(q, q)

            with act.Fori(1, ROUNDS - 1) as r:
                for k in range(PER_ROUND):
                    s = r * PER_ROUND + (STEPS0 + k)
                    gate(k, s)
                    hidden_hi(k - 1, s - 1)
                    c = k // 4 + AHEAD
                    if k % 4 == 1:
                        split_hi(c % SETS, r + (1 + c // SETS), free_at(r, c))
            for k in TAIL:
                if k < PER_ROUND:
                    gate(k, LAST_S + k)
                if k <= PER_ROUND:
                    hidden_hi(k - 1, LAST_S + k - 1)
                c = k + AHEAD
                if c < SETS:
                    split_hi(c, ROUNDS, LAST_S - PER_ROUND + 4 * c + 3)
                for q in quads_at(k, Y_OUT):
                    act.wait_ge(s_down, LAST_S + 4 * q + 4)
                    a.copy(y_t[:, q, :], ps[:, acc_bank(q), :]).then_inc(s_yt, 1)

        @block.vector
        def _(dve):
            v = nc.vector
            steps = [0]

            def link(ins):
                steps[0] += 1
                ins.then_inc(s_dve, 1)
                dve.wait_ge(s_dve, steps[0])

            def statistics(k, src):
                if made[0]:
                    dve.wait_ge(s_var, made[0])
                made[0] += 1
                for t in range(4):
                    ins = v.bn_stats(stats[:, t, :], src(t))
                link(ins)
                for t in range(4):
                    ins = v.bn_aggr(mv[:, k, t, :], stats[:, t, :])
                ins.then_inc(s_var, 1)

            made = [0]

            def scale(n, k, src, dst):
                dve.wait_ge(s_rstd, n + 1)
                for t in range(4):
                    ins = v.tensor_scalar(dst(t), src(t), mv[:, k, t, 0:1], rstd[:, k, t:t + 1],
                                          ALU.subtract, ALU.mult)
                return ins

            def flat(t3):
                return t3.rearrange("p a b -> p (a b)")

            def latent_lo(q):
                own = slice(512 * q, 512 * q + 512)
                dve.wait_ge(s_lhi, q + 1)
                link(v.tensor_tensor(lat_lo[:, own], ps[:, 1, :], lat_hi[:, own], ALU.subtract))
                v.tensor_copy(lat_hl[R:2 * R, own], lat_lo[R:2 * R, own]).then_inc(s_llo, 1)

            def row_max(q, r):
                i = keys_of(q) - 4 + r
                first = 2 + (r % 2 if q % QPB == 0 else 0)
                rows = ps[:, first:4, :].rearrange("p a b -> p (a b)")
                dve.wait_ge(s_rows, 4 * q + r + 1)
                v.tensor_reduce(neg_max[:, 4 * q + r:4 * q + r + 1], rows[:, 0:P * i + P],
                                AX.X, ALU.max, negate=True).then_inc(s_max, 1)

            def max_row_lo(q):
                dve.wait_ge(s_mhi, q + 1)
                low = neg_max_t[R:P, q % 2, :]
                v.tensor_tensor(low, ps[R:P, 1, :], low, ALU.subtract).then_inc(s_mlo, 1)

            def divide(q, h):
                dve.wait_ge(s_pv, 2 * q + h + 1)
                bank = ps[:, 7, :].rearrange("p (t c) -> p t c", t=2)
                inv = row_sum_inv[:, 4 * q + 2 * h:4 * q + 2 * h + 2]
                link(v.reciprocal(inv, bank[:, :, C]))
                for t in range(2):
                    ins = v.scalar_tensor_tensor(
                        out=att[:, q % 2, 2 * h + t, :], in0=bank[:, t, 0:C],
                        scalar=inv[:, t:t + 1], in1=bo_sb[:], op0=ALU.mult, op1=ALU.add)
                ins.then_inc(s_att, 1)

            def norm_x(q):
                scale(NORMS.index(("S", q)), q % 2, lambda t: x_sb[:, 4 * q + t, :],
                      lambda t: xn[:, q % 2, t, :]).then_inc(s_xn, 1)

            def add_attention(q):
                own = slice(4 * q, 4 * q + 4)
                link(scale(NORMS.index(("D", q)), 2 + q % 2, lambda t: att[:, q % 2, t, :],
                           lambda t: x1_sb[:, 4 * q + t, :]))
                link(v.tensor_tensor(x1_sb[:, own, :], x1_sb[:, own, :], x_sb[:, own, :],
                                     ALU.add))
                statistics(2 + q % 2, lambda t: x1_sb[:, 4 * q + t, :])

            def norm_x1(q):
                if q >= 1:
                    dve.wait_ge(s_x2p, q)
                scale(NORMS.index(("X", q)), 2 + q % 2, lambda t: x1_sb[:, 4 * q + t, :],
                      lambda t: xn2[:, t, :]).then_inc(s_xn2, 1)

            tt = v.tensor_tensor

            def score_groups(q):
                k = q % 2
                dve.wait_ge(s_choice, q + 1)
                if q:
                    dve.wait_ge(s_gin, q)
                grp = choice[:, k].rearrange("p t (g k) -> p (t g) k", k=GE)
                tt(big[0][:], grp[:, :, 0:4], grp[:, :, 4:8], ALU.max)
                link(tt(small[0][:], grp[:, :, 0:4], grp[:, :, 4:8], ALU.min))
                for n in range(2):
                    w = 2 >> n
                    b0, b1 = big[n][:, :, 0:w], big[n][:, :, w:2 * w]
                    tt(big[n + 1][:], b0, b1, ALU.max)
                    tt(low_big[:, :, 0:w], b0, b1, ALU.min)
                    link(tt(small[n + 1][:], small[n][:, :, 0:w], small[n][:, :, w:2 * w],
                            ALU.max))
                    link(tt(small[n + 1][:], small[n + 1][:], low_big[:, :, 0:w], ALU.max))
                link(tt(group_score[:, :, :].rearrange("p t g -> p (t g)"), big[2][:, :, 0],
                        small[2][:, :, 0], ALU.add))
            def choose_groups(q):
                if q:
                    dve.wait_ge(s_masked, q)
                for t in range(4):
                    ins = v.max(group_top[:, t, :], group_score[:, t, :])
                link(ins)
                link(v.tensor_copy(group_find[:, :, 0:TOP_GROUPS], group_top[:, :, 0:TOP_GROUPS]))
                for t in range(4):
                    ins = v.match_replace(group_left[:, t, :], group_find[:, t, :],
                                          group_score[:, t, :], TAKEN)
                link(ins)
                tt(group_in[:], group_left[:], group_score[:], ALU.not_equal).then_inc(s_gin, 1)

            def choose_experts(q):
                dve.wait_ge(s_masked, q + 1)
                for t in range(4):
                    ins = v.max(top8[:, t, :], masked[:, t, :])
                link(ins)
                for t in range(4):
                    ins = v.match_replace(left[:, t, :], top8[:, t, :], masked[:, t, :], TAKEN)
                link(ins)

            def weigh_experts(q):
                k = q % 2
                link(v.tensor_tensor(left[:], left[:], masked[:], ALU.not_equal))
                link(v.tensor_tensor(left[:], left[:], scores[:, k], ALU.mult))
                link(v.tensor_reduce(wsum[:], left[:], AX.X, ALU.add))
                link(v.tensor_scalar(wsum[:], wsum[:], 1e-20, 1.0 / ROUTED_SCALE, ALU.add,
                                     ALU.mult))
                link(v.reciprocal(winv[:], wsum[:]))
                if q >= 1:
                    dve.wait_ge(s_rx, 2 * q)
                v.tensor_tensor(route[:], left[:],
                                winv[:, :].unsqueeze(2).to_broadcast([P, 4, E]),
                                ALU.mult).then_inc(s_route, 1)

            def split_lo(c, n, loads, used):
                dve.wait_ge(s_wl[c], 16 * loads)
                dve.wait_ge(s_whi, n + 1)
                dve.wait_ge(s_down, used + 1)
                v.tensor_tensor(w_lo[:, c, :], w_raw[:, c, :], w_hi[:, c, :],
                                ALU.subtract).then_inc(s_wlo, 1)

            def weigh(k, s, q, group):
                dve.wait_ge(s_up, s + 1)
                if later(s, 2):
                    dve.wait_ge(s_hid, s - 1)
                v.tensor_tensor(up_w[:, k % 2, :], ps[:, gate_bank(k) + 1, :],
                                route_w[:, group, 512 * q:512 * q + 512],
                                ALU.mult).then_inc(s_upw, 1)

            def hidden_lo(k, s):
                dve.wait_ge(s_hhi, s + 1)
                if later(s, 2):
                    dve.wait_ge(s_down, s - 1)
                v.tensor_tensor(hid_lo[:, k % 2, :], hid[:, k % 2, :], hid_hi[:, k % 2, :],
                                ALU.subtract).then_inc(s_hlo, 1)

            for what, q, n in ORDER:
                if what == "S":
                    dve.wait_ge(s_x[q], 16)
                    if q >= 2:
                        dve.wait_ge(s_xn, q - 1)
                    statistics(q % 2, lambda t: x_sb[:, 4 * q + t, :])
                elif what == "P" and not norm_on_pool(what, q):
                    norm_x(q)
                elif what == "Q":
                    latent_lo(q)
                    if q == 0:
                        dve.wait_ge(s_wvop, 2)
                        link(tt(bo_sb[:], bo_sb[:], ps[:, 6, 0:C], ALU.add))
                elif what == "A":
                    row_max(q, n)
                elif what == "M":
                    max_row_lo(q)
                elif what == "C":
                    divide(q, n)
                elif what == "D":
                    dve.wait_ge(s_att, 2 * q + 2)
                    if q >= 2:
                        dve.wait_ge(s_xn2, q - 1)
                    statistics(2 + q % 2, lambda t: att[:, q % 2, t, :])
                elif what == "X":
                    add_attention(q)
                elif what == "Y" and not norm_on_pool(what, q):
                    norm_x1(q)
                elif what == "H":
                    score_groups(q)
                elif what == "J":
                    choose_groups(q)
                elif what == "I":
                    choose_experts(q)
                elif what == "O":
                    weigh_experts(q)
                elif what == "R" and q >= SETS:
                    split_lo(q % SETS, q, q // SETS + 1,
                             last_user(q - SETS))
                elif what == "Z" and is_routed(q):
                    quad, c, _ = FIRST[q]
                    dve.wait_ge(s_rw, SETS * (quad + 1))
                    weigh(q, q, quad, c)
                elif what == "Z":
                    dve.wait_ge(s_hid0, 1)
                    dve.wait_ge(s_gated, q + 1)
                    dve.wait_ge(s_up, q + 1)
                    if q >= 1:
                        dve.wait_ge(s_hid, q)
                    if q >= 2:
                        dve.wait_ge(s_hlo, q - 1)
                    tt(hid[0:SROWS, q % 2, :], gated[0:SROWS, q % 2, :],
                       ps[0:SROWS, gate_bank(q) + 1, :], ALU.mult).then_inc(s_hid, 1)
                elif what == "W":
                    hidden_lo(q, q)

            dve.wait_ge(s_rw, SETS * QUADS)

            with dve.Fori(1, ROUNDS - 1) as r:
                for k in range(PER_ROUND):
                    s = r * PER_ROUND + (STEPS0 + k)
                    weigh(k, s, k % 4, k // 4)
                    hidden_lo(k - 1, s - 1)
                    c = k // 4 + AHEAD
                    if k % 4 == 1:
                        split_lo(c % SETS, r * SETS + c, r + (1 + c // SETS), free_at(r, c))

            for k in TAIL:
                if k < PER_ROUND:
                    weigh(k, LAST_S + k, k // 4, k % 4)
                if k <= PER_ROUND:
                    hidden_lo(k - 1, LAST_S + k - 1)
                c = k + AHEAD
                if c < SETS:
                    split_lo(c, (ROUNDS - 1) * SETS + c, ROUNDS,
                             LAST_S - PER_ROUND + 4 * c + 3)
                for q in quads_at(k, Y_STATS):
                    dve.wait_ge(s_yp, q + 1)
                    dve.wait_ge(s_xn2, QUADS)
                    statistics(2 + q % 2, lambda t: ps[:, acc_bank(q), P * t:P * t + P])
                for q in quads_at(k, Y_NORM):
                    own = slice(4 * q, 4 * q + 4)
                    link(scale(len(NORMS) + q, 2 + q % 2,
                               lambda t: ps[:, acc_bank(q), P * t:P * t + P],
                               lambda t: x_sb[:, 4 * q + t, :]))
                    v.tensor_tensor(flat(x_sb[:, own, :]), flat(x_sb[:, own, :]),
                                    flat(x1_sb[:, own, :]), ALU.add).then_inc(s_y, 1)

        @block.tensor
        def _(pe):
            t_ = nc.tensor

            def bank_free(at, kinds, last):
                st = stage_before(at, kinds)
                if st:
                    pe.wait_ge(last[st[0]], st[1] + 1)

            def turn_xn(q, at):
                bank_free(at, "PE", {"P": s_xn_t, "E": s_xhi})
                pe.wait_ge(s_xn, q + 1)
                for t in range(4):
                    mm = t_.transpose(ps[:, 0, P * t:P * t + P], xn[:, q % 2, t, :], ident[:])
                mm.then_inc(s_xn_tp, 1)

            def bank7_free(at):
                st = stage_before(at, "VC")
                if st:
                    what, q, h = st
                    if what == "C":
                        pe.wait_ge(s_att, 2 * q + h + 1)
                    else:
                        pe.wait_ge(s_v, q + 1)

            def bank1_free(at):
                bank_free(at, "QMF", {"Q": s_llo, "M": s_mlo, "F": s_sc})

            def banks23_user(at):
                users = [st for st in ORDER[:at]
                         if st[0] in "AG" or (st[0] == "Z" and st[1] % 2 == 1)]
                return users[-1] if users else None

            def banks23_free(at, rows=None):
                st = banks23_user(at)
                if st and st[0] == "Z":
                    pe.wait_ge(s_gated, st[1] + 1)
                    if is_routed(st[1]):
                        pe.wait_ge(s_upw, weighted(st[1]))
                    else:
                        pe.wait_ge(s_hid, st[1] + 1)
                elif st and st[0] == "A":
                    done = 4 * st[1] + st[2] + 1
                    if rows and rows[0] % QPB == 0 and rows[1] > 0:
                        done -= 1
                    if done:
                        pe.wait_ge(s_max, done)
                elif st:
                    pe.wait_ge(s_rw, SETS * st[1] + 2 * st[2] + 2)

            def latent(q, at):
                pe.wait_ge(s_xn_t, q + 1)
                bank1_free(at)
                t_.matmul(ps[:, 1, :], wb_sb[:], xn_t[:, q % 2, :], start=True,
                          stop=True).then_inc(s_lat, 1)

            def values(q, at):
                pe.wait_ge(s_xn_t, q + 1)
                pe.wait_ge(s_wvo, 1)
                bank7_free(at)
                for t in range(4):
                    mm = t_.matmul(ps[:, 7, P * t:P * t + P], xn_t[:, q % 2, P * t:P * t + P],
                                   wvo_sb[:], start=True, stop=True)
                mm.then_inc(s_vp, 1)

            def score_rows(q, r, at):
                base = (q // QPB) * seq
                i = keys_of(q) - 4 + r
                banks23_free(at, (q, r))
                pe.wait_ge(s_llo, q + 1)
                first = 2 + (r % 2 if q % QPB == 0 else 0)
                own = lat_hl[:, 512 * q + P * r:512 * q + P * r + P]
                for lo in range(0, P * i + P, 512):
                    w = min(512, P * i + P - lo)
                    keys = slice(base + lo, base + lo + w)
                    o = ps[:, first + lo // 512, :]
                    t_.matmul(o[:, 0:w], own, lat_hi[:, keys], start=True, stop=False)
                    mm = t_.matmul(o[:, 0:w], own, lat_lo[:, keys], start=False, stop=True)
                mm = t_.matmul(o[:, w - P:w], ident_r[:], mask_rows, start=False, stop=True,
                               skip_group_check=True)
                mm.then_inc(s_rows, 1)

            def max_row(q, at):
                bank1_free(at)
                pe.wait_ge(s_max, 4 * q + 4)
                for r in range(4):
                    mm = t_.matmul(ps[:, 1, P * r:P * r + P],
                                   neg_max[:, 4 * q + r:4 * q + r + 1].to_broadcast([P, P]),
                                   ident[:], start=True, stop=True)
                mm.then_inc(s_mrow, 1)

            def score_cols(q, j):
                base = (q // QPB) * seq
                n = cols_before(q) + j
                d = j - (keys_of(q) - 4)
                lo = P * max(d, 0)
                pe.wait_ge(s_mlo, q + 1)
                if n >= 2:
                    pe.wait_ge(s_exp, n - 1)
                o = ps[:, 4 + n % 2, lo:512]
                keys = lat_hl[:, base + P * j:base + P * j + P]
                cols = slice(512 * q + lo, 512 * q + 512)
                t_.matmul(o, keys, lat_hi[:, cols], start=True, stop=False)
                t_.matmul(o, keys, lat_lo[:, cols], start=False, stop=False)
                mm = t_.matmul(o, pick[:], neg_max_t[:, q % 2, lo:512], start=False, stop=True)
                if d >= 0:
                    mm = t_.matmul(ps[:, 4 + n % 2, lo:lo + P], ident_r[:], mask_cols,
                                   start=False, stop=True, skip_group_check=True)
                mm.then_inc(s_cols, 1)

            def weigh_values(q, h, at):
                pe.wait_ge(s_v, q + 1)
                pe.wait_ge(s_exp, cols_before(q) + keys_of(q))
                bank7_free(at)
                for r in (2 * h, 2 * h + 1):
                    i = keys_of(q) - 4 + r
                    for j in range(i + 1):
                        mm = t_.matmul(ps[:, 7, 256 * (r % 2):256 * (r % 2) + C + 1],
                                       exp_t[:, q % 2, j, P * r:P * r + P],
                                       vals[:, (q // QPB) * TPB + j, 0:C + 1], start=(j == 0),
                                       stop=(j == i))
                mm.then_inc(s_pv, 1)

            def expert_input(q, at):
                bank_free(at, "PE", {"P": s_xn_t, "E": s_xhi})
                pe.wait_ge(s_xn2, q + 1)
                for t in range(4):
                    mm = t_.transpose(ps[:, 0, P * t:P * t + P], xn2[:, t, :], ident[:])
                mm.then_inc(s_x2p, 1)

            def logits(q, at):
                bank1_free(at)
                pe.wait_ge(s_x2, q + 1)
                for t in range(4):
                    mm = t_.matmul(ps[:, 1, E * t:E * t + E], x2_t[:, P * t:P * t + P], gw_sb[:],
                                   start=True, stop=True)
                mm.then_inc(s_lg, 1)

            def turn_route(q, h, at):
                pe.wait_ge(s_rx, 2 * q + h + 1)
                follows = banks23_user(at) == ("G", q, 0)
                if not follows:
                    banks23_free(at)
                for g in (2 * h, 2 * h + 1):
                    n = SETS * q + g
                    if follows:
                        pe.wait_ge(s_rw, n - 1)
                    for t in range(4):
                        mm = t_.transpose(
                            ps[:, 2 + n % 2, P * t:P * t + P],
                            route_x[:, t, PER_CHUNK * g:PER_CHUNK * (g + 1), :]
                            .rearrange("p e k -> p (e k)"), ident[:])
                    mm.then_inc(s_rtp, 1)

            def products(out_, hi, lo, mhi, mlo, start, stop):
                t_.matmul(out_, hi, mhi, start=start, stop=False)
                t_.matmul(out_, hi, mlo, start=False, stop=False)
                return t_.matmul(out_, lo, mhi, start=False, stop=stop)

            def gate_up(k, s, q, whi, wlo, n):
                g = gate_bank(k)
                cols = slice(512 * q, 512 * q + 512)
                if later(s, 2):
                    pe.wait_ge(s_gated, s - 1)
                products(ps[0:n, g, :], whi[:, 0:n], wlo[:, 0:n], x_hi[:, cols],
                         x_lo[:, cols], True, True).then_inc(s_gate, 1)
                if later(s, 2):
                    if is_routed(s - 2):
                        pe.wait_ge(s_upw, weighted(s - 2))
                    else:
                        pe.wait_ge(s_hid, s - 1)
                products(ps[0:n, g + 1, :], whi[:, n:2 * n], wlo[:, n:2 * n],
                         x_hi[:, cols], x_lo[:, cols], True, True).then_inc(s_up, 1)

            def down(k, s, q, whi, wlo, n, start=False, stop=False):
                pe.wait_ge(s_hlo, s + 1)
                products(ps[:, acc_bank(q), :], whi[0:n, WD:WD + P], wlo[0:n, WD:WD + P],
                         hid_hi[0:n, k % 2, :], hid_lo[0:n, k % 2, :], start,
                         stop).then_inc(s_down, 1)

            def first_weights(s):
                _, c, routed = FIRST[s]
                return (w_hi[:, c, :], w_lo[:, c, :], P) if routed else (
                    sh_hi[:, c, :], sh_lo[:, c, :], SROWS)

            def first_gate_up(s, at):
                q, c, routed = FIRST[s]
                if s == 0:
                    pe.wait_ge(s_exp, cols_before(QUADS))
                if routed:
                    pe.wait_ge(s_wlo, c + 1)
                else:
                    pe.wait_ge(s_shlo, 2 * (c + 1))
                pe.wait_ge(s_xlo, q + 1)
                if s % 2 == 1:
                    banks23_free(at)
                gate_up(s, s, q, *first_weights(s))

            def first_down(s):
                q, c, routed = FIRST[s]
                starts = not routed and c == 0
                if starts:
                    if q == 0:
                        pe.wait_ge(s_att, 1)
                    elif q == 1:
                        pe.wait_ge(s_att, 2 * QUADS)
                    elif q == 2:
                        pe.wait_ge(s_xhi, QUADS)
                    else:
                        pe.wait_ge(s_sc, QUADS)
                down(s, s, q, *first_weights(s), start=starts)

            pe.wait_ge(s_w, 16 * W_LOADS)
            t_.matmul(ps[:, 7, 0:C], wv_sb[:], wo_sb[:], start=True, stop=True).then_inc(s_wvop, 1)
            t_.matmul(ps[:, 6, 0:C], bv_sb[:, 0:1].to_broadcast([P, P]), wo_sb[:], start=True,
                      stop=True).then_inc(s_wvop, 1)
            pe.wait_ge(s_const, 1)
            for at, (what, q, n) in enumerate(ORDER):
                if what == "P":
                    turn_xn(q, at)
                elif what == "Q":
                    latent(q, at)
                elif what == "V":
                    values(q, at)
                elif what == "A":
                    score_rows(q, n, at)
                elif what == "M":
                    max_row(q, at)
                elif what == "B":
                    score_cols(q, n)
                elif what == "C":
                    weigh_values(q, n, at)
                elif what == "E":
                    expert_input(q, at)
                elif what == "G":
                    turn_route(q, n, at)
                elif what == "F":
                    logits(q, at)
                elif what == "Z":
                    first_gate_up(q, at)
                elif what == "W" and q >= 1:
                    first_down(q - 1)

            pe.wait_ge(s_rw, SETS * QUADS)

            def round_steps(r, first=False):
                for k in range(PER_ROUND):
                    s = r * PER_ROUND + (STEPS0 + k)
                    c = k // 4
                    if k % 4 == 0:
                        pe.wait_ge(s_wlo, r * SETS + (c + 1))
                    gate_up(k, s, k % 4, w_hi[:, c, :], w_lo[:, c, :], P)
                    if first and k < LAG:
                        first_down(FIRST_STEPS - LAG + k)
                    else:
                        kd = (k - LAG) % PER_ROUND
                        down(kd, s - LAG, kd % 4, w_hi[:, kd // 4, :], w_lo[:, kd // 4, :], P)

            round_steps(1, first=True)
            with pe.Fori(2, ROUNDS - 1) as r:
                round_steps(r)
            for k in TAIL:
                if k < PER_ROUND:
                    c = k % 4
                    if k < SETS:
                        pe.wait_ge(s_wlo, (ROUNDS - 1) * SETS + c + 1)
                    gate_up(k, LAST_S + k, k // 4, w_hi[:, c, :], w_lo[:, c, :], P)
                kd = k - LAG
                if kd < 0:
                    down(kd, LAST_S + kd, kd % 4, w_hi[:, SETS - 1, :], w_lo[:, SETS - 1, :], P)
                elif kd < PER_ROUND:
                    c = kd % 4
                    down(kd, LAST_S + kd, kd // 4, w_hi[:, c, :], w_lo[:, c, :], P,
                         stop=(c == SETS - 1))
                for q in quads_at(k, Y_TURN):
                    pe.wait_ge(s_yt, q + 1)
                    for t in range(4):
                        mm = t_.transpose(ps[:, acc_bank(q), P * t:P * t + P],
                                          y_t[:, q, P * t:P * t + P], ident[:])
                    mm.then_inc(s_yp, 1)




def kernel(L0_attn_hidden_states, L0_attn_W_basis, L0_attn_W_v, L0_attn_b_v, L0_attn_W_o,
           L0_attn_b_o, L0_ffn_gate_w, L0_ffn_gate_bias, L0_ffn_Wg, L0_ffn_Wu, L0_ffn_Wd,
           L0_ffn_Sg, L0_ffn_Su, L0_ffn_Sd):
    import concourse.bacc as bacc
    from concourse.bass_utils import run_bass_kernel_spmd

    E, I, H = L0_ffn_Wg.shape
    sets, rounds = E // PER_CHUNK, I // PACK
    up = [np.asarray(w).reshape(sets, PER_CHUNK, rounds, PACK, H).transpose(2, 0, 4, 1, 3)
          .reshape(rounds, sets, H, P) for w in (L0_ffn_Wg, L0_ffn_Wu)]
    down = (np.asarray(L0_ffn_Wd).reshape(sets, PER_CHUNK, H, rounds, PACK)
            .transpose(3, 0, 1, 4, 2).reshape(rounds, sets, P, H))
    shared = 2
    s_up = [np.asarray(w).reshape(shared, -1, H).transpose(0, 2, 1) for w in (L0_ffn_Sg, L0_ffn_Su)]
    arrays = {
        "x": np.asarray(L0_attn_hidden_states),
        "w_basis_t": np.asarray(L0_attn_W_basis).T,
        "w_v": np.asarray(L0_attn_W_v),
        "b_v": np.asarray(L0_attn_b_v)[:, None],
        "w_o_t": np.asarray(L0_attn_W_o).T,
        "b_o": np.asarray(L0_attn_b_o)[None, :],
        "gate_w_t": np.asarray(L0_ffn_gate_w).T,
        "gate_bias": np.asarray(L0_ffn_gate_bias)[None, :],
        "w_experts": np.concatenate([*up, down], axis=3),
        "w_shared_up": np.concatenate(s_up, axis=2),
        "w_shared_down": np.asarray(L0_ffn_Sd).T.reshape(shared, -1, H),
    }
    arrays = {k: np.ascontiguousarray(a) for k, a in arrays.items()}
    nc = bacc.Bacc("TRN2", target_bir_lowering=False, num_devices=1)
    args = [nc.dram_tensor(f"in_{k}", a.shape, F32, kind="ExternalInput").ap()
            for k, a in arrays.items()]
    out = nc.dram_tensor("out", arrays["x"].shape, F32, kind="ExternalOutput").ap()
    build(nc, *args, out)
    r = run_bass_kernel_spmd(nc, [{f"in_{k}": a for k, a in arrays.items()}], core_ids=[0])
    return r.results[0]["out"]
```
